# Optimizing a Trainium2 kernel written in Bass

```python
import numpy as np
import jax
import jax.numpy as jnp

def _softmax(x, axis=-1):
    return jax.nn.softmax(x, axis=axis)

def _gelu(x):
    return jax.nn.gelu(x, approximate=True)

def _silu(x):
    return jax.nn.silu(x)

def _sigmoid(x):
    return jax.nn.sigmoid(x)

def _layernorm(x, axis=-1, eps=1e-05):
    m = jnp.mean(x, axis=axis, keepdims=True)
    v = jnp.var(x, axis=axis, keepdims=True)
    return (x - m) / jnp.sqrt(v + eps)

def _scatter_add(tgt, idx, src, axis=0):
    return tgt.at[idx].add(src)

def _segment_sum(src, seg, n):
    return jax.ops.segment_sum(src, seg, n)
kernel_name = 'mk_adj_resnorm_d1_adj_r2_140dd7'

def setup_inputs(seed: int=0):
    np.random.seed(seed)
    _w = jnp.asarray

    def _rec_inputs():
        import jax
        import jax.numpy as jnp
        _gk = jax.random.key(seed)
        x = 7.22e-05 + 1 * jax.random.normal(jax.random.fold_in(_gk, 1), (32, 256, 256), jnp.float32)
        _w = (1.0 + jnp.arange(256, dtype=jnp.float32)) ** (-0.5)
        _w = _w / _w.mean()
        _pij = jnp.clip(0.03125 * _w[:, None] * _w[None, :], 0.0, 1.0)
        _a = jax.random.uniform(jax.random.fold_in(_gk, 2), (32, 256, 256)) < _pij
        _a = jnp.logical_or(_a, jnp.swapaxes(_a, -1, -2))
        _a = jnp.logical_or(_a, jnp.eye(256, dtype=bool))
        _af = _a.astype(jnp.float32)
        _af = _af * jax.random.uniform(jax.random.fold_in(_gk, 3), (32, 256, 256), jnp.float32, 0.05, 1)
        adj = _af
        return (x, adj)
    x, adj = _rec_inputs()

    def _L0_gnn_setup():
        import jax, jax.numpy as jnp
        import numpy as np
        EPS_LN = 1e-05

        def hypergraph_conv(x, adj, W, b):
            N, C, _ = adj.shape
            H = (adj != 0).astype(x.dtype)
            w = adj.reshape(N, -1)[:, :C]
            xw = jnp.einsum('ncd,hd->nch', x, W)
            Dn = jnp.einsum('nce,ne->nc', H, w)
            Dn = jnp.where(Dn > 0, 1.0 / Dn, 0.0)
            Be = H.sum(axis=1)
            Be = jnp.where(Be > 0, 1.0 / Be, 0.0)
            m = Be[:, :, None] * jnp.einsum('nce,nch->neh', H, xw)
            out = Dn[:, :, None] * jnp.einsum('nce,neh->nch', H, m)
            return out + b

        def layer_norm(x, g, b):
            mu = jnp.mean(x, axis=-1, keepdims=True)
            var = jnp.var(x, axis=-1, keepdims=True)
            return (x - mu) * jax.lax.rsqrt(var + EPS_LN) * g + b
        key = jax.random.key(seed)
        ks = jax.random.split(key, 4)
        N, C, Din, Dh, Dout = (16, 512, 256, 512, 256)
        x = jax.random.normal(ks[0], (N, C, Din), dtype=jnp.float32)
        adj = jax.random.uniform(ks[1], (N, C, C), dtype=jnp.float32, minval=0.1, maxval=1.0)
        W1 = jax.random.normal(ks[2], (Dh, Din), dtype=jnp.float32) * (1.0 / np.sqrt(Din))
        b1 = jnp.zeros((Dh,), dtype=jnp.float32)
        gamma = jnp.ones((Dh,), dtype=jnp.float32)
        beta = jnp.zeros((Dh,), dtype=jnp.float32)
        W2 = jax.random.normal(ks[3], (Dout, Dh), dtype=jnp.float32) * (1.0 / np.sqrt(Dh))
        b2 = jnp.zeros((Dout,), dtype=jnp.float32)
        return {'x': x, 'adj': adj, 'W1': W1, 'b1': b1, 'gamma': gamma, 'beta': beta, 'W2': W2, 'b2': b2}
    _L0_gnn_all = _L0_gnn_setup()
    _L0_gnn_in = {k: v for k, v in _L0_gnn_all.items() if k in ('W1', 'b1', 'gamma', 'beta', 'W2', 'b2')}
    del _L0_gnn_all
    return {'x': x, 'adj': adj, 'L0_gnn_W1': _L0_gnn_in['W1'], 'L0_gnn_b1': _L0_gnn_in['b1'], 'L0_gnn_gamma': _L0_gnn_in['gamma'], 'L0_gnn_beta': _L0_gnn_in['beta'], 'L0_gnn_W2': _L0_gnn_in['W2'], 'L0_gnn_b2': _L0_gnn_in['b2']}

def reference(x, adj, L0_gnn_W1, L0_gnn_b1, L0_gnn_gamma, L0_gnn_beta, L0_gnn_W2, L0_gnn_b2):
    import jax
    import jax.numpy as jnp

    def _L0_gnn_ref(x, adj, W1, b1, gamma, beta, W2, b2):
        import jax, jax.numpy as jnp
        import numpy as np
        EPS_LN = 1e-05

        def hypergraph_conv(x, adj, W, b):
            N, C, _ = adj.shape
            H = (adj != 0).astype(x.dtype)
            w = adj.reshape(N, -1)[:, :C]
            xw = jnp.einsum('ncd,hd->nch', x, W)
            Dn = jnp.einsum('nce,ne->nc', H, w)
            Dn = jnp.where(Dn > 0, 1.0 / Dn, 0.0)
            Be = H.sum(axis=1)
            Be = jnp.where(Be > 0, 1.0 / Be, 0.0)
            m = Be[:, :, None] * jnp.einsum('nce,nch->neh', H, xw)
            out = Dn[:, :, None] * jnp.einsum('nce,neh->nch', H, m)
            return out + b

        def layer_norm(x, g, b):
            mu = jnp.mean(x, axis=-1, keepdims=True)
            var = jnp.var(x, axis=-1, keepdims=True)
            return (x - mu) * jax.lax.rsqrt(var + EPS_LN) * g + b
        h = jax.nn.relu(hypergraph_conv(x, adj, W1, b1))
        h = layer_norm(h, gamma, beta)
        y = hypergraph_conv(h, adj, W2, b2)
        return y + x
    x = _layernorm(x + _L0_gnn_ref(x, adj, L0_gnn_W1, L0_gnn_b1, L0_gnn_gamma, L0_gnn_beta, L0_gnn_W2, L0_gnn_b2), axis=-1)
    return x

_drawn_inputs = setup_inputs


def setup_inputs(seed=0):
    import zlib

    import numpy as np

    out = dict(_drawn_inputs(seed))
    spreads = {'L0_gnn_b1': (0.0, 0.1),
     'L0_gnn_gamma': (1.0, 0.2),
     'L0_gnn_beta': (0.0, 0.1),
     'L0_gnn_b2': (0.0, 0.1)}
    factors = {}
    for name, (base, spread) in spreads.items():
        noise = np.random.default_rng([zlib.crc32(name.encode()), seed]).standard_normal(out[name].shape)
        drawn = base * np.exp(spread * noise) if base else spread * noise
        out[name] = jnp.asarray(drawn.astype(out[name].dtype))
    for name, factor in factors.items():
        out[name] = (out[name] * factor).astype(out[name].dtype)
    return out
```

```python
import concourse.bass as bass
from concourse import mybir
from contextlib import ExitStack


def hypergraph_kernel(nc, x, adj, w1, b1, gamma, beta, w2, b2, out):
    f32 = mybir.dt.float32
    f32r = mybir.dt.float32r
    ALU = mybir.AluOpType
    ACT = mybir.ActivationFunctionType
    AX = mybir.AxisListType

    P = nc.NUM_PARTITIONS
    N, C, D = x.shape
    DH = w1.shape[0]
    B = C // P
    HB = DH // P
    EPS = 1e-5
    TINY = 1.2e-38
    RING = 3
    LOOPS = (N - 2) // RING
    C_LOADS = 4 + B
    W2T_DONE = 2 * B
    assert (B, HB) == (2, 4) and 1 + RING * LOOPS == N - 1

    x_rows = x.rearrange("n (p b) d -> n p b d", b=B)
    adj_rows = adj.rearrange("n (p b) e -> n p b e", b=B)
    out_rows = out.rearrange("n (p b) d -> n p b d", b=B)

    ctx = ExitStack()
    with ctx:
        def sb(name, shape, dt=f32):
            return ctx.enter_context(nc.sbuf_tensor(name, shape, dt))

        def ps(name, shape):
            return ctx.enter_context(nc.psum_tensor(name, shape, f32))

        def sem(name):
            return ctx.enter_context(nc.semaphore(name))

        ident = sb("ident", [P, P])
        w1_nat = sb("w1_nat", [P, HB, D])
        w2_nat = sb("w2_nat", [P, B, DH])
        w1t_hi = sb("w1t_hi", [P, B, DH], f32r)
        w1t_lo = sb("w1t_lo", [P, B, DH], f32r)
        w2t = sb("w2t", [P, HB, D])
        w2g_hi = sb("w2g_hi", [P, HB, D], f32r)
        w2g_lo = sb("w2g_lo", [P, HB, D], f32r)
        gamma_col = sb("gamma_col", [P, HB])
        beta_col = sb("beta_col", [P, HB])
        beta_wide = sb("beta_wide", [P, HB, P])
        ones = sb("ones", [P, P])
        b1_all = sb("b1_all", [P, DH])
        b2_all = sb("b2_all", [P, B, D])
        bias_rows = sb("bias_rows", [P, D], f32r)
        averager = sb("averager", [P, P], f32r)
        row0_nat = sb("row0_nat", [N, C])
        row0_hi = sb("row0_hi", [P, B, N, 2], f32r)
        minus_half = sb("minus_half", [P, B])

        adj_in = sb("adj_in", [P, RING, B, C])
        x_in = sb("x_in", [P, RING, B, D])
        H = sb("H", [P, RING, B, C], f32r)
        HT = sb("HT", [P, RING, B, C], f32r)
        skip = sb("skip", [P, RING, B, D])
        counts = sb("counts", [P, RING, 2, B])
        recips = sb("recips", [P, RING, 2, B])
        dn = sb("dn", [P, RING, B])
        clamp = sb("clamp", [P, 2, B])
        x_hi = sb("x_hi", [P, B, D], f32r)
        x_lo = sb("x_lo", [P, B, D], f32r)
        m_hi = sb("m_hi", [P, B, D], f32r)
        m_lo = sb("m_lo", [P, B, D], f32r)
        a_hi = sb("a_hi", [P, B, C], f32r)
        a_lo = sb("a_lo", [P, B, C], f32r)
        pre = sb("pre", [P, B, DH])
        act_h = sb("act_h", [P, B, DH])
        norm_h = sb("norm_h", [P, B, DH])
        bn_h = sb("bn_h", [P, B, 6])
        mv_h = sb("mv_h", [P, B, 2])
        var_h = sb("var_h", [P, B])
        rstd_h = sb("rstd_h", [P, B])
        minus_mean_h = sb("minus_mean_h", [P, B])
        t_hi = sb("t_hi", [P, B, HB, P], f32r)
        t_lo = sb("t_lo", [P, B, HB, P], f32r)
        y_hi = sb("y_hi", [P, B, D], f32r)
        y_lo = sb("y_lo", [P, B, D], f32r)
        p_hi = sb("p_hi", [P, B, D], f32r)
        p_lo = sb("p_lo", [P, B, D], f32r)
        res = sb("res", [P, B, D])
        bn_o = sb("bn_o", [P, B, 6])
        mv_o = sb("mv_o", [P, B, 2])
        var_o = sb("var_o", [P, B])
        rstd_o = sb("rstd_o", [P, B])
        minus_mean_o = sb("minus_mean_o", [P, B])
        fin = sb("fin", [P, B, D])

        ht_ps = ps("ht_ps", [P, B, C])
        deg_ps = ps("deg_ps", [P, B, C])
        ma_ps = ps("ma_ps", [P, B, C])
        ypo_ps = ps("ypo_ps", [P, B, D])
        z_ps = ps("z_ps", [P, B, DH])
        t_ps = ps("t_ps", [P, B, HB, P])

        w_in = sem("w_in")
        c_in = sem("c_in")
        setup_pool = sem("setup_pool")
        setup_pe = sem("setup_pe")
        setup_act = sem("setup_act")
        setup_dve = sem("setup_dve")
        row0_steps = sem("row0_steps")
        bias_steps = sem("bias_steps")
        adj_loaded = [sem(f"adj_loaded{r}") for r in range(RING)]
        x_loaded = [sem(f"x_loaded{r}") for r in range(RING)]
        h_made = sem("h_made")
        xhi_made = sem("xhi_made")
        xlo_made = sem("xlo_made")
        skip_half = sem("skip_half")
        skip_made = sem("skip_made")
        ht_turned = sem("ht_turned")
        ht_made = sem("ht_made")
        m_done = sem("m_done")
        deg_done = sem("deg_done")
        deg_summed = sem("deg_summed")
        clamped = sem("clamped")
        recip_made = sem("recip_made")
        dn_made = sem("dn_made")
        mhi_made = sem("mhi_made")
        mlo_made = sem("mlo_made")
        a_done = sem("a_done")
        ahi_made = sem("ahi_made")
        alo_made = sem("alo_made")
        z_done = sem("z_done")
        pre_made = sem("pre_made")
        relu_made = sem("relu_made")
        bnh_made = sem("bnh_made")
        mvh_made = sem("mvh_made")
        rstdh_steps = sem("rstdh_steps")
        norm_made = sem("norm_made")
        t_turned = sem("t_turned")
        thi_made = sem("thi_made")
        tlo_made = sem("tlo_made")
        y_done = sem("y_done")
        yhi_made = sem("yhi_made")
        ylo_made = sem("ylo_made")
        p_done = sem("p_done")
        phi_made = sem("phi_made")
        plo_made = sem("plo_made")
        o_done = sem("o_done")
        res_made = sem("res_made")
        bno_made = sem("bno_made")
        mvo_made = sem("mvo_made")
        rstdo_steps = sem("rstdo_steps")
        fin_made = sem("fin_made")
        stored = sem("stored")

        def settled(engine, value):
            return value if isinstance(value, int) else engine.to_reg(value)

        def read(cut):
            return cut.bitcast(f32)

        block = ctx.enter_context(nc.Block())

        @block.sync
        def _(sp):
            sp.dma_start(w1_nat[:], w1.rearrange("(b p) d -> p b d", p=P)).then_inc(w_in, 16)
            sp.dma_start(w2_nat[:], w2.rearrange("(b p) h -> p b h", p=P)).then_inc(w_in, 16)

            def load(n, r, again):
                if again:
                    sp.wait_ge(h_made, n - RING + 1)
                sp.dma_start(adj_in[:, r], adj_rows[n]).then_inc(adj_loaded[r], 16)
                if again:
                    sp.wait_ge(xhi_made, n - RING + 1)
                    sp.wait_ge(xlo_made, n - RING + 1)
                    sp.wait_ge(skip_made, n - RING + 1)
                sp.dma_start(x_in[:, r], x_rows[n]).then_inc(x_loaded[r], 16)

            def store(n):
                sp.wait_ge(fin_made, 2 * (n + 1))
                sp.dma_start(out_rows[n], fin[:]).then_inc(stored, 16)

            for n in range(RING):
                load(n, n, False)
            with sp.Fori(1, N // RING) as j:
                for c in range(RING):
                    load(RING * j + c, c, True)
                    store(RING * j + c - RING)
            for n in range(RING * (N // RING), N):
                load(n, n % RING, True)
                store(n - RING)
            for n in range(N - RING, N):
                store(n)
            sp.wait_ge(stored, 16 * N)

        @block.gpsimd
        def _(pool):
            pool.memset(ident[:], 0.0).then_inc(setup_pool, 1)
            pool.memset(ones[:], 1.0).then_inc(setup_pool, 1)
            pool.memset(minus_half[:], -0.5).then_inc(setup_pool, 1)
            pool.wait_ge(setup_pool, 3)
            pool.affine_select(out=ident[:], in_=ident[:], compare_op=ALU.not_equal, fill=1.0, base=0,
                               pattern=[[-1, P]], channel_multiplier=1).then_inc(setup_pool, 1)
            pool.wait_ge(c_in, 16 * C_LOADS)

            def cut_x(n, r, arrived):
                pool.wait_ge(x_loaded[r], arrived)
                pool.wait_ge(xhi_made, n + 1)
                pool.wait_ge(m_done, n)
                pool.tensor_tensor(x_lo[:], x_in[:, r], read(x_hi[:]), ALU.subtract).then_inc(xlo_made, 1)

            def add_skip(n, r, reused):
                if reused:
                    pool.wait_ge(res_made, B * (n - 1))
                pool.tensor_tensor(skip[:, r], x_in[:, r], b2_all[:], ALU.add).then_inc(skip_half, 1)
                pool.wait_ge(skip_half, n + 1)
                pool.tensor_tensor(skip[:, r], skip[:, r], x_in[:, r], ALU.add).then_inc(skip_made, 1)

            def normalise_hidden(n, b, reused):
                k = B * n + b
                made = settled(pool, k + 1)
                pool.wait_ge(setup_pool, 1)
                pool.wait_ge(mvh_made, made)
                pool.tensor_scalar(var_h[:, b:b + 1], mv_h[:, b, 1:2], EPS, None, ALU.add).then_inc(rstdh_steps, 1)
                pool.wait_ge(rstdh_steps, 3 * k + 1)
                pool.tensor_tensor(rstd_h[:, b:b + 1], var_h[:, b:b + 1], minus_half[:, 0:1],
                                   ALU.pow).then_inc(rstdh_steps, 1)
                pool.tensor_scalar(minus_mean_h[:, b:b + 1], mv_h[:, b, 0:1], -1.0, None,
                                   ALU.mult).then_inc(rstdh_steps, 1)
                steps, used = settled(pool, 3 * k + 3), settled(pool, k - 1)
                pool.wait_ge(setup_pool, 1)
                pool.wait_ge(rstdh_steps, steps)
                if reused:
                    pool.wait_ge(t_turned, used)
                pool.tensor_scalar(norm_h[:, b], act_h[:, b], minus_mean_h[:, b:b + 1], rstd_h[:, b:b + 1],
                                   ALU.add, ALU.mult).then_inc(norm_made, 1)

            def normalise_out(n):
                made = settled(pool, B * (n + 1))
                pool.wait_ge(setup_pool, 1)
                pool.wait_ge(mvo_made, made)
                pool.tensor_scalar(var_o[:], mv_o[:, :, 1], EPS, None, ALU.add).then_inc(rstdo_steps, 1)
                pool.wait_ge(rstdo_steps, 3 * n + 1)
                pool.tensor_tensor(rstd_o[:], var_o[:], minus_half[:], ALU.pow).then_inc(rstdo_steps, 1)
                pool.tensor_scalar(minus_mean_o[:], mv_o[:, :, 0], -1.0, None, ALU.mult).then_inc(rstdo_steps, 1)
                steps, left = settled(pool, 3 * n + 3), settled(pool, 16 * n)
                pool.wait_ge(setup_pool, 1)
                pool.wait_ge(rstdo_steps, steps)
                pool.wait_ge(stored, left)
                for b in range(B):
                    pool.tensor_scalar(fin[:, b], res[:, b], minus_mean_o[:, b:b + 1], rstd_o[:, b:b + 1],
                                       ALU.add, ALU.mult).then_inc(fin_made, 1)

            def step(j, c, first=False, last=False):
                i = RING * j + c
                if not last:
                    cut_x(i + 1, (c + 1) % RING, 16 * (j + (c + 1) // RING + 1))
                add_skip(i, c % RING, not first)
                normalise_hidden(i, 0, not first)
                normalise_hidden(i, 1, not first)
                if not first:
                    normalise_out(i - 1)

            cut_x(0, 0, 16)
            step(0, 0, first=True)
            with pool.Fori(0, LOOPS) as j:
                for c in range(1, RING + 1):
                    step(j, c)
            step(LOOPS, 1, last=True)
            normalise_out(N - 1)

        @block.scalar
        def _(act):
            act.dma_start(b1_all[:], b1.partition_broadcast(P)).then_inc(c_in, 16)
            for b in range(B):
                act.dma_start(b2_all[:, b], b2.partition_broadcast(P)).then_inc(c_in, 16)
            act.dma_start(gamma_col[:], gamma.rearrange("(b p) -> p b", p=P),
                          allow_slow_non_contiguous=True).then_inc(c_in, 16)
            act.dma_start(beta_col[:], beta.rearrange("(b p) -> p b", p=P),
                          allow_slow_non_contiguous=True).then_inc(c_in, 16)
            act.dma_start(row0_nat[:], adj[:, 0, :]).then_inc(c_in, 16)

            def cut_x(n, r, arrived):
                act.wait_ge(x_loaded[r], arrived)
                act.wait_ge(m_done, n)
                act.activation(x_hi[:], x_in[:, r], ACT.Copy).then_inc(xhi_made, 1)

            def keep_ht(n, r):
                act.wait_ge(ht_turned, n + 1)
                for b in range(B):
                    act.activation(HT[:, r, b], ht_ps[:, b], ACT.Copy,
                                   accum_out=counts[:, r, 0, b:b + 1]).then_inc(ht_made, 1)

            def cut_m(n, r):
                act.wait_ge(m_done, n + 1)
                act.wait_ge(recip_made, n + 1)
                act.wait_ge(a_done, n)
                for b in range(B):
                    act.activation(m_hi[:, b], ma_ps[:, b], ACT.Copy,
                                   scale=recips[:, r, 0, b:b + 1]).then_inc(mhi_made, 1)

            def cut_a(n):
                act.wait_ge(a_done, n + 1)
                act.wait_ge(z_done, B * n)
                act.activation(a_hi[:], ma_ps[:], ACT.Copy).then_inc(ahi_made, 1)

            def relu(n, b, reused):
                act.wait_ge(pre_made, B * n + b + 1)
                if reused:
                    act.wait_ge(norm_made, B * n + b - 1)
                act.activation(act_h[:, b], pre[:, b], ACT.Relu).then_inc(relu_made, 1)

            def cut_t(n, b):
                act.wait_ge(t_turned, B * n + b + 1)
                act.wait_ge(y_done, n)
                act.activation(t_hi[:, b], t_ps[:, b], ACT.Copy).then_inc(thi_made, 1)

            def cut_y(n):
                act.wait_ge(y_done, n + 1)
                act.wait_ge(p_done, n)
                act.activation(y_hi[:], ypo_ps[:], ACT.Copy).then_inc(yhi_made, 1)

            def cut_p(n, r):
                act.wait_ge(p_done, n + 1)
                act.wait_ge(o_done, n)
                for b in range(B):
                    act.activation(p_hi[:, b], ypo_ps[:, b], ACT.Copy,
                                   scale=recips[:, r, 0, b:b + 1]).then_inc(phi_made, 1)

            def step(j, c, first=False, last=False):
                i = RING * j + c
                if not first:
                    cut_y(i - 1)
                if not last:
                    cut_x(i + 1, (c + 1) % RING, 16 * (j + (c + 1) // RING + 1))
                relu(i, 0, not first)
                relu(i, 1, not first)
                if not first:
                    cut_p(i - 1, (c - 1) % RING)
                if not last:
                    keep_ht(i + 1, (c + 1) % RING)
                    cut_m(i + 1, (c + 1) % RING)
                cut_t(i, 0)
                cut_t(i, 1)
                if not last:
                    cut_a(i + 1)

            cut_x(0, 0, 16)
            for b in range(B):
                act.wait_ge(setup_pe, b + 1)
                act.activation(w1t_hi[:, b], z_ps[:, b], ACT.Copy).then_inc(setup_act, 1)
            act.wait_ge(c_in, 16 * C_LOADS)
            act.wait_ge(setup_dve, W2T_DONE)
            for b in range(HB):
                act.activation(w2g_hi[:, b], w2t[:, b], ACT.Copy,
                               scale=gamma_col[:, b:b + 1]).then_inc(setup_act, 1)
            keep_ht(0, 0)
            cut_m(0, 0)
            cut_a(0)
            step(0, 0, first=True)
            with act.Fori(0, LOOPS) as j:
                for c in range(1, RING + 1):
                    step(j, c)
            step(LOOPS, 1, last=True)
            cut_y(N - 1)
            cut_p(N - 1, (N - 1) % RING)

        @block.vector
        def _(dve):
            def make_h(n, r, arrived, reused):
                dve.wait_ge(adj_loaded[r], arrived)
                if reused:
                    dve.wait_ge(p_done, n - RING + 1)
                dve.tensor_scalar(H[:, r], adj_in[:, r], 0.0, None, ALU.not_equal).then_inc(h_made, 1)

            def reciprocals(n, r):
                dve.wait_ge(deg_done, n + 1)
                dve.tensor_reduce(counts[:, r, 1], deg_ps[:, :, 0:2], AX.X, ALU.add).then_inc(deg_summed, 1)
                dve.wait_ge(deg_summed, n + 1)
                dve.wait_ge(ht_made, B * (n + 1))
                dve.tensor_scalar(clamp[:], counts[:, r], TINY, None, ALU.max).then_inc(clamped, 1)
                dve.wait_ge(clamped, n + 1)
                dve.reciprocal(recips[:, r], clamp[:]).then_inc(recip_made, 1)
                dve.wait_ge(recip_made, n + 1)
                dve.scalar_tensor_tensor(out=dn[:, r], in0=counts[:, r, 1], scalar=0.0, in1=recips[:, r, 1],
                                         op0=ALU.is_gt, op1=ALU.mult).then_inc(dn_made, 1)

            def cut_m(n, r):
                dve.wait_ge(mhi_made, B * (n + 1))
                for b in range(B):
                    dve.scalar_tensor_tensor(out=m_lo[:, b], in0=ma_ps[:, b], scalar=recips[:, r, 0, b:b + 1],
                                             in1=read(m_hi[:, b]), op0=ALU.mult,
                                             op1=ALU.subtract).then_inc(mlo_made, 1)

            def cut_a(n):
                dve.wait_ge(ahi_made, n + 1)
                dve.tensor_tensor(a_lo[:], ma_ps[:], read(a_hi[:]), ALU.subtract).then_inc(alo_made, 1)

            def scale_z(n, r, b, reused):
                dve.wait_ge(z_done, B * n + b + 1)
                dve.wait_ge(dn_made, n + 1)
                if reused:
                    dve.wait_ge(relu_made, B * n + b - 1)
                dve.scalar_tensor_tensor(out=pre[:, b], in0=z_ps[:, b], scalar=dn[:, r, b:b + 1],
                                         in1=b1_all[:], op0=ALU.mult, op1=ALU.add).then_inc(pre_made, 1)

            def hidden_moments(n, b, reused):
                k = B * n + b + 1
                dve.wait_ge(relu_made, k)
                dve.bn_stats(bn_h[:, b], act_h[:, b]).then_inc(bnh_made, 1)
                used = settled(dve, k - B)
                k = settled(dve, k)
                dve.wait_ge(setup_dve, 1)
                dve.wait_ge(bnh_made, k)
                if reused:
                    dve.wait_ge(norm_made, used)
                dve.bn_aggr(mv_h[:, b], bn_h[:, b]).then_inc(mvh_made, 1)

            def cut_t(n, b):
                dve.wait_ge(thi_made, B * n + b + 1)
                dve.tensor_tensor(t_lo[:, b], t_ps[:, b], read(t_hi[:, b]), ALU.subtract).then_inc(tlo_made, 1)

            def cut_y(n):
                dve.wait_ge(yhi_made, n + 1)
                dve.tensor_tensor(y_lo[:], ypo_ps[:], read(y_hi[:]), ALU.subtract).then_inc(ylo_made, 1)

            def cut_p(n, r):
                dve.wait_ge(phi_made, B * (n + 1))
                for b in range(B):
                    dve.scalar_tensor_tensor(out=p_lo[:, b], in0=ypo_ps[:, b], scalar=recips[:, r, 0, b:b + 1],
                                             in1=read(p_hi[:, b]), op0=ALU.mult,
                                             op1=ALU.subtract).then_inc(plo_made, 1)

            def finish(n, r):
                dve.wait_ge(o_done, n + 1)
                dve.wait_ge(skip_made, n + 1)
                dve.wait_ge(fin_made, B * n)
                for b in range(B):
                    dve.scalar_tensor_tensor(out=res[:, b], in0=ypo_ps[:, b], scalar=dn[:, r, b:b + 1],
                                             in1=skip[:, r, b], op0=ALU.mult, op1=ALU.add).then_inc(res_made, 1)
                for b in range(B):
                    dve.wait_ge(res_made, B * n + b + 1)
                    dve.bn_stats(bn_o[:, b], res[:, b]).then_inc(bno_made, 1)
                for b in range(B):
                    k = settled(dve, B * n + b + 1)
                    dve.wait_ge(setup_dve, 1)
                    dve.wait_ge(bno_made, k)
                    dve.bn_aggr(mv_o[:, b], bn_o[:, b]).then_inc(mvo_made, 1)

            def step(j, c, first=False, last=False):
                i = RING * j + c
                if not first:
                    cut_y(i - 1)
                if not last:
                    make_h(i + 1, (c + 1) % RING, 16 * (j + (c + 1) // RING + 1), not first)
                scale_z(i, c % RING, 0, not first)
                hidden_moments(i, 0, not first)
                scale_z(i, c % RING, 1, not first)
                hidden_moments(i, 1, not first)
                if not first:
                    cut_p(i - 1, (c - 1) % RING)
                if not last:
                    reciprocals(i + 1, (c + 1) % RING)
                    cut_m(i + 1, (c + 1) % RING)
                cut_t(i, 0)
                cut_t(i, 1)
                if not last:
                    cut_a(i + 1)
                if not first:
                    finish(i - 1, (c - 1) % RING)

            make_h(0, 0, 16, False)
            for b in range(B):
                dve.wait_ge(setup_act, b + 1)
                dve.tensor_tensor(w1t_lo[:, b], z_ps[:, b], read(w1t_hi[:, b]), ALU.subtract).then_inc(setup_dve, 1)
            for b in range(B):
                dve.wait_ge(setup_pe, B + b + 1)
                dve.tensor_copy(w2t[:, :, b * P:(b + 1) * P], t_ps[:, b]).then_inc(setup_dve, 1)
            dve.wait_ge(setup_pe, 2 * B + 1)
            for b in range(B):
                turned = deg_ps[:, b, 0:N]
                dve.tensor_copy(row0_hi[:, b, :, 0], turned).then_inc(row0_steps, 1)
                dve.wait_ge(row0_steps, 2 * b + 1)
                dve.tensor_tensor(row0_hi[:, b, :, 1], turned, read(row0_hi[:, b, :, 0]),
                                  ALU.subtract).then_inc(row0_steps, 1)
            dve.wait_ge(c_in, 16 * C_LOADS)
            dve.wait_ge(setup_pool, 2)
            for b in range(HB):
                dve.tensor_scalar(beta_wide[:, b], ones[:], beta_col[:, b:b + 1], None, ALU.mult).then_inc(setup_dve, 1)
            dve.tensor_scalar(averager[:], ones[:], 2.0 / P, None, ALU.mult).then_inc(setup_dve, 1)
            for b in range(HB):
                dve.wait_ge(setup_act, B + b + 1)
                dve.scalar_tensor_tensor(out=w2g_lo[:, b], in0=w2t[:, b], scalar=gamma_col[:, b:b + 1],
                                         in1=read(w2g_hi[:, b]), op0=ALU.mult,
                                         op1=ALU.subtract).then_inc(setup_dve, 1)
            dve.wait_ge(setup_pe, 2 * B + 2)
            dve.tensor_copy(bias_rows[:], ypo_ps[:, 0]).then_inc(bias_steps, 1)
            dve.wait_ge(bias_steps, 1)
            dve.tensor_tensor(bias_rows[P // 2:P], ypo_ps[P // 2:P, 0], read(bias_rows[P // 2:P]),
                              ALU.subtract).then_inc(bias_steps, 1)
            reciprocals(0, 0)
            cut_m(0, 0)
            cut_a(0)
            step(0, 0, first=True)
            with dve.Fori(0, LOOPS) as j:
                for c in range(1, RING + 1):
                    step(j, c)
            step(LOOPS, 1, last=True)
            cut_y(N - 1)
            cut_p(N - 1, (N - 1) % RING)
            finish(N - 1, (N - 1) % RING)

        @block.tensor
        def _(pe):
            def product(out, pairs, start=True, stop=True):
                for k, (lhs, rhs) in enumerate(pairs):
                    mm = pe.matmul(out, lhs, rhs, start=start and k == 0, stop=stop and k == len(pairs) - 1)
                return mm

            def turn_h(n, r):
                pe.wait_ge(h_made, n + 1)
                pe.wait_ge(ht_made, B * n)
                for e in range(B):
                    for b in range(B):
                        mm = pe.transpose(ht_ps[:, e, b * P:(b + 1) * P], read(H[:, r, b, e * P:(e + 1) * P]),
                                          ident[:])
                mm.then_inc(ht_turned, 1)

            def edge_sums(n, r):
                pe.wait_ge(xhi_made, n + 1)
                pe.wait_ge(alo_made, n)
                for e in range(B):
                    if e == 0:
                        for b in range(B):
                            pe.matmul(ma_ps[:, e], H[:, r, b, e * P:(e + 1) * P], x_hi[:, b], start=(b == 0), stop=False)
                        pe.wait_ge(xlo_made, n + 1)
                        pairs = [(H[:, r, b, 0:P], x_lo[:, b]) for b in range(B)]
                        product(ma_ps[:, e], pairs, start=False)
                    else:
                        mm = product(ma_ps[:, e], [(H[:, r, b, e * P:(e + 1) * P], part[:, b])
                                                   for part in (x_hi, x_lo) for b in range(B)])
                mm.then_inc(m_done, 1)

            def degrees(n, r):
                pe.wait_ge(ht_made, B * (n + 1))
                pe.wait_ge(deg_summed, n)
                for b in range(B):
                    mm = product(deg_ps[:, b, 0:2], [(HT[:, r, e, b * P:(b + 1) * P], row0_hi[:, e, n, :])
                                                     for e in range(B)])
                mm.then_inc(deg_done, 1)

            def node_sums(n, r):
                pe.wait_ge(mhi_made, B * (n + 1))
                pe.wait_ge(mlo_made, B * (n + 1))
                for d in range(B):
                    mm = product(ma_ps[:, d], [(part[:, e, d * P:(d + 1) * P], HT[:, r, e])
                                               for part in (m_hi, m_lo) for e in range(B)])
                mm.then_inc(a_done, 1)

            def hidden(n, reused):
                pe.wait_ge(ahi_made, n + 1)
                pe.wait_ge(alo_made, n + 1)
                for b in range(B):
                    if reused:
                        pe.wait_ge(pre_made, B * n + b - 1)
                    mm = product(z_ps[:, b], [(a[:, d, b * P:(b + 1) * P], w[:, d])
                                              for a, w in ((a_hi, w1t_hi), (a_hi, w1t_lo), (a_lo, w1t_hi))
                                              for d in range(B)])
                    mm.then_inc(z_done, 1)

            def turn_t(n, b, reused):
                pe.wait_ge(norm_made, B * n + b + 1)
                if reused:
                    pe.wait_ge(tlo_made, B * n + b - 1)
                for h in range(HB):
                    mm = pe.transpose(t_ps[:, b, h], norm_h[:, b, h * P:(h + 1) * P], ident[:])
                mm.then_inc(t_turned, 1)

            def project(n):
                pe.wait_ge(res_made, B * n)
                for b in range(B):
                    pe.matmul(ypo_ps[:, b], averager[:], bias_rows[:], start=True, stop=False)
                    pe.wait_ge(thi_made, B * n + b + 1)
                    product(ypo_ps[:, b], [(t_hi[:, b, h], w[:, h]) for w in (w2g_hi, w2g_lo) for h in range(HB)],
                            start=False, stop=False)
                    pe.wait_ge(tlo_made, B * n + b + 1)
                    mm = product(ypo_ps[:, b], [(t_lo[:, b, h], w2g_hi[:, h]) for h in range(HB)], start=False)
                mm.then_inc(y_done, 1)

            def edge_sums_2(n, r):
                pe.wait_ge(yhi_made, n + 1)
                pe.wait_ge(ylo_made, n + 1)
                for e in range(B):
                    mm = product(ypo_ps[:, e], [(H[:, r, b, e * P:(e + 1) * P], part[:, b])
                                                for part in (y_hi, y_lo) for b in range(B)])
                mm.then_inc(p_done, 1)

            def node_sums_2(n, r):
                pe.wait_ge(phi_made, B * (n + 1))
                pe.wait_ge(plo_made, B * (n + 1))
                for b in range(B):
                    mm = product(ypo_ps[:, b], [(HT[:, r, e, b * P:(b + 1) * P], part[:, e])
                                                for part in (p_hi, p_lo) for e in range(B)])
                mm.then_inc(o_done, 1)

            def step(j, c, first=False, last=False):
                i = RING * j + c
                now, after, before = c % RING, (c + 1) % RING, (c - 1) % RING
                hidden(i, not first)
                if not first:
                    edge_sums_2(i - 1, before)
                if not last:
                    turn_h(i + 1, after)
                    edge_sums(i + 1, after)
                    degrees(i + 1, after)
                if not first:
                    node_sums_2(i - 1, before)
                turn_t(i, 0, not first)
                turn_t(i, 1, not first)
                if not last:
                    node_sums(i + 1, after)
                project(i)

            pe.wait_ge(w_in, 32)
            pe.wait_ge(setup_pool, 4)
            for b in range(B):
                for h in range(HB):
                    mm = pe.transpose(z_ps[:, b, h * P:(h + 1) * P], w1_nat[:, h, b * P:(b + 1) * P], ident[:])
                mm.then_inc(setup_pe, 1)
            for b in range(B):
                for h in range(HB):
                    mm = pe.transpose(t_ps[:, b, h], w2_nat[:, b, h * P:(h + 1) * P], ident[:])
                mm.then_inc(setup_pe, 1)
            pe.wait_ge(c_in, 16 * C_LOADS)
            for b in range(B):
                mm = pe.transpose(deg_ps[:, b, 0:N], row0_nat[:, b * P:(b + 1) * P], ident[0:N, 0:N])
            mm.then_inc(setup_pe, 1)
            pe.wait_ge(setup_dve, W2T_DONE + HB + 1)
            mm = product(ypo_ps[:, 0], [(beta_wide[:, h], w2t[:, h]) for h in range(HB)])
            mm.then_inc(setup_pe, 1)

            turn_h(0, 0)
            edge_sums(0, 0)
            pe.wait_ge(row0_steps, 2 * B)
            degrees(0, 0)
            node_sums(0, 0)
            pe.wait_ge(setup_dve, W2T_DONE + 2 * HB + 1)
            pe.wait_ge(bias_steps, 2)
            step(0, 0, first=True)
            with pe.Fori(0, LOOPS) as j:
                for c in range(1, RING + 1):
                    step(j, c)
            step(LOOPS, 1, last=True)
            edge_sums_2(N - 1, (N - 1) % RING)
            node_sums_2(N - 1, (N - 1) % RING)


_INS = ["x", "adj", "L0_gnn_W1", "L0_gnn_b1", "L0_gnn_gamma", "L0_gnn_beta", "L0_gnn_W2", "L0_gnn_b2"]


def kernel(**inputs):
    import numpy as _np
    import concourse.bacc as _bacc
    from concourse import mybir as _mybir
    from concourse.bass_utils import run_bass_kernel_spmd as _run

    nc = _bacc.Bacc("TRN2", target_bir_lowering=False, num_devices=1)
    arrays, args = {}, []
    for name in _INS:
        a = _np.ascontiguousarray(inputs[name])
        arrays[f"in_{name}"] = a
        args.append(nc.dram_tensor(f"in_{name}", a.shape, _mybir.dt.from_np(a.dtype), kind="ExternalInput").ap())
    shape = arrays["in_x"].shape
    out = nc.dram_tensor("out_0", shape, _mybir.dt.float32, kind="ExternalOutput").ap()
    hypergraph_kernel(nc, *args, out)
    r = _run(nc, [arrays], core_ids=[0])
    return r.results[0]["out_0"]
```

```python
import concourse.bass as bass
from concourse import mybir
from contextlib import ExitStack


def hypergraph_kernel(nc, x, adj, w1, b1, gamma, beta, w2, b2, out):
    f32 = mybir.dt.float32
    f32r = mybir.dt.float32r
    ALU = mybir.AluOpType
    ACT = mybir.ActivationFunctionType
    AX = mybir.AxisListType

    P = nc.NUM_PARTITIONS
    N, C, D = x.shape
    DH = w1.shape[0]
    B = C // P
    HB = DH // P
    EPS = 1e-5
    TINY = 1.2e-38
    RING = 4
    FIRST = 3
    LOOPS = (N - FIRST) // RING
    LAST = FIRST + RING * LOOPS
    C_LOADS = 4 + B
    W2T_DONE = 2 * B
    assert (B, HB) == (2, 4) and N % RING == 0 and LAST == N - 1

    x_rows = x.rearrange("n (p b) d -> n p b d", b=B)
    adj_rows = adj.rearrange("n (p b) e -> n p b e", b=B)
    out_rows = out.rearrange("n (p b) d -> n p b d", b=B)

    ctx = ExitStack()
    with ctx:
        def sb(name, shape, dt=f32):
            return ctx.enter_context(nc.sbuf_tensor(name, shape, dt))

        def ps(name, shape):
            return ctx.enter_context(nc.psum_tensor(name, shape, f32))

        def sem(name):
            return ctx.enter_context(nc.semaphore(name))

        ident = sb("ident", [P, P])
        w1_nat = sb("w1_nat", [P, HB, D])
        w2_nat = sb("w2_nat", [P, B, DH])
        w1t_hi = sb("w1t_hi", [P, B, DH], f32r)
        w1t_lo = sb("w1t_lo", [P, B, DH], f32r)
        w2t = sb("w2t", [P, HB, D])
        w2g_hi = sb("w2g_hi", [P, HB, D], f32r)
        w2g_lo = sb("w2g_lo", [P, HB, D], f32r)
        gamma_col = sb("gamma_col", [P, HB])
        beta_col = sb("beta_col", [P, HB])
        beta_wide = sb("beta_wide", [P, HB, P])
        ones = sb("ones", [P, P])
        b1_all = sb("b1_all", [P, DH])
        b2_all = sb("b2_all", [P, B, D])
        bias_rows = sb("bias_rows", [P, D], f32r)
        averager = sb("averager", [P, P], f32r)
        row0_nat = sb("row0_nat", [N, C])
        row0_cut = sb("row0_cut", [P, B, N, 2], f32r)
        minus_half = sb("minus_half", [P, B])

        adj_in = sb("adj_in", [P, RING, B, C])
        x_in = sb("x_in", [P, RING, B, D])
        H = sb("H", [P, RING, B, C], f32r)
        HT = sb("HT", [P, RING, B, C], f32r)
        skip = sb("skip", [P, RING, B, D])
        counts = sb("counts", [P, RING, 2, B])
        recips = sb("recips", [P, RING, 2, B])
        dn = sb("dn", [P, RING, B])
        clamp = sb("clamp", [P, 2, B])
        x_hi = sb("x_hi", [P, B, D], f32r)
        x_lo = sb("x_lo", [P, B, D], f32r)
        m_hi = sb("m_hi", [P, B, D], f32r)
        m_lo = sb("m_lo", [P, B, D], f32r)
        a_hi = sb("a_hi", [P, B, C], f32r)
        a_lo = sb("a_lo", [P, B, C], f32r)
        pre = sb("pre", [P, B, DH])
        act_h = sb("act_h", [P, B, DH])
        norm_h = sb("norm_h", [P, B, DH])
        bn_h = sb("bn_h", [P, B, 6])
        mv_h = sb("mv_h", [P, B, 2])
        var_h = sb("var_h", [P, B])
        rstd_h = sb("rstd_h", [P, B])
        minus_mean_h = sb("minus_mean_h", [P, B])
        t_hi = sb("t_hi", [P, B, HB, P], f32r)
        t_lo = sb("t_lo", [P, B, HB, P], f32r)
        y_hi = sb("y_hi", [P, B, D], f32r)
        y_lo = sb("y_lo", [P, B, D], f32r)
        p_hi = sb("p_hi", [P, B, D], f32r)
        p_lo = sb("p_lo", [P, B, D], f32r)
        res = sb("res", [P, B, D])
        bn_o = sb("bn_o", [P, B, 6])
        mv_o = sb("mv_o", [P, B, 2])
        var_o = sb("var_o", [P, B])
        rstd_o = sb("rstd_o", [P, B])
        minus_mean_o = sb("minus_mean_o", [P, B])
        fin = sb("fin", [P, B, D])

        ht_ps = ps("ht_ps", [P, B, C])
        ma_ps = ps("ma_ps", [P, B, C])
        y_ps = ps("y_ps", [P, B, D])
        po_ps = ps("po_ps", [P, B, D])
        z_ps = ps("z_ps", [P, B, DH])
        t_ps = ps("t_ps", [P, B, HB, P])

        w_in = sem("w_in")
        c_in = sem("c_in")
        setup_pool = sem("setup_pool")
        setup_pe = sem("setup_pe")
        setup_act = sem("setup_act")
        setup_dve = sem("setup_dve")
        row0_steps = sem("row0_steps")
        bias_steps = sem("bias_steps")
        adj_loaded = [sem(f"adj_loaded{r}") for r in range(RING)]
        x_loaded = [sem(f"x_loaded{r}") for r in range(RING)]
        h_made = sem("h_made")
        xhi_made = sem("xhi_made")
        xlo_made = sem("xlo_made")
        skip_half = sem("skip_half")
        skip_made = sem("skip_made")
        ht_turned = sem("ht_turned")
        ht_made = sem("ht_made")
        m_done = sem("m_done")
        deg_done = sem("deg_done")
        deg_summed = sem("deg_summed")
        be_clamped = sem("be_clamped")
        be_made = sem("be_made")
        deg_clamped = sem("deg_clamped")
        deg_inverted = sem("deg_inverted")
        dn_made = sem("dn_made")
        mhi_made = sem("mhi_made")
        mlo_made = sem("mlo_made")
        a_done = sem("a_done")
        ahi_made = sem("ahi_made")
        alo_made = sem("alo_made")
        z_done = sem("z_done")
        pre_made = sem("pre_made")
        relu_made = sem("relu_made")
        bnh_made = sem("bnh_made")
        mvh_made = sem("mvh_made")
        rstdh_steps = sem("rstdh_steps")
        norm_made = sem("norm_made")
        t_turned = sem("t_turned")
        thi_made = sem("thi_made")
        tlo_made = sem("tlo_made")
        y_done = sem("y_done")
        yhi_made = sem("yhi_made")
        ylo_made = sem("ylo_made")
        p_done = sem("p_done")
        phi_made = sem("phi_made")
        plo_made = sem("plo_made")
        o_done = sem("o_done")
        res_made = sem("res_made")
        bno_made = sem("bno_made")
        mvo_made = sem("mvo_made")
        rstdo_steps = sem("rstdo_steps")
        fin_made = sem("fin_made")
        stored = sem("stored")

        def settled(engine, value):
            return value if isinstance(value, int) else engine.to_reg(value)

        def read(cut):
            return cut.bitcast(f32)

        block = ctx.enter_context(nc.Block())

        @block.sync
        def _(sp):
            sp.dma_start(w1_nat[:], w1.rearrange("(b p) d -> p b d", p=P)).then_inc(w_in, 16)
            sp.dma_start(w2_nat[:], w2.rearrange("(b p) h -> p b h", p=P)).then_inc(w_in, 16)

            def load(n, r, again):
                if again:
                    sp.wait_ge(h_made, n - RING + 1)
                sp.dma_start(adj_in[:, r], adj_rows[n]).then_inc(adj_loaded[r], 16)
                if again:
                    sp.wait_ge(xhi_made, n - RING + 1)
                    sp.wait_ge(xlo_made, n - RING + 1)
                    sp.wait_ge(skip_made, n - RING + 1)
                sp.dma_start(x_in[:, r], x_rows[n]).then_inc(x_loaded[r], 16)

            def store(n):
                sp.wait_ge(fin_made, 2 * (n + 1))
                sp.dma_start(out_rows[n], fin[:]).then_inc(stored, 16)

            for n in range(RING):
                load(n, n, False)
            with sp.Fori(1, N // RING) as j:
                for c in range(RING):
                    load(RING * j + c, c, True)
                    store(RING * j + c - RING)
            for n in range(N - RING, N):
                store(n)
            sp.wait_ge(stored, 16 * N)

        @block.gpsimd
        def _(pool):
            pool.memset(ident[:], 0.0).then_inc(setup_pool, 1)
            pool.memset(ones[:], 1.0).then_inc(setup_pool, 1)
            pool.memset(minus_half[:], -0.5).then_inc(setup_pool, 1)
            pool.wait_ge(setup_pool, 3)
            pool.affine_select(out=ident[:], in_=ident[:], compare_op=ALU.not_equal, fill=1.0, base=0,
                               pattern=[[-1, P]], channel_multiplier=1).then_inc(setup_pool, 1)
            pool.wait_ge(c_in, 16 * C_LOADS)

            def cut_x(n, r, arrived):
                pool.wait_ge(x_loaded[r], arrived)
                pool.wait_ge(xhi_made, n + 1)
                pool.tensor_tensor(x_lo[:], x_in[:, r], read(x_hi[:]), ALU.subtract).then_inc(xlo_made, 1)

            def add_skip(n, r):
                pool.tensor_tensor(skip[:, r], x_in[:, r], b2_all[:], ALU.add).then_inc(skip_half, 1)
                pool.wait_ge(skip_half, n + 1)
                pool.tensor_tensor(skip[:, r], skip[:, r], x_in[:, r], ALU.add).then_inc(skip_made, 1)

            def normalise_hidden(n, b):
                k = B * n + b
                made = settled(pool, k + 1)
                pool.wait_ge(setup_pool, 1)
                pool.wait_ge(mvh_made, made)
                pool.tensor_scalar(var_h[:, b:b + 1], mv_h[:, b, 1:2], EPS, None, ALU.add).then_inc(rstdh_steps, 1)
                pool.wait_ge(rstdh_steps, 3 * k + 1)
                pool.tensor_tensor(rstd_h[:, b:b + 1], var_h[:, b:b + 1], minus_half[:, 0:1],
                                   ALU.pow).then_inc(rstdh_steps, 1)
                pool.tensor_scalar(minus_mean_h[:, b:b + 1], mv_h[:, b, 0:1], -1.0, None,
                                   ALU.mult).then_inc(rstdh_steps, 1)
                steps = settled(pool, 3 * k + 3)
                pool.wait_ge(setup_pool, 1)
                pool.wait_ge(rstdh_steps, steps)
                pool.tensor_scalar(norm_h[:, b], act_h[:, b], minus_mean_h[:, b:b + 1], rstd_h[:, b:b + 1],
                                   ALU.add, ALU.mult).then_inc(norm_made, 1)

            def normalise_out(n):
                made = settled(pool, B * (n + 1))
                pool.wait_ge(setup_pool, 1)
                pool.wait_ge(mvo_made, made)
                pool.tensor_scalar(var_o[:], mv_o[:, :, 1], EPS, None, ALU.add).then_inc(rstdo_steps, 1)
                pool.wait_ge(rstdo_steps, 3 * n + 1)
                pool.tensor_tensor(rstd_o[:], var_o[:], minus_half[:], ALU.pow).then_inc(rstdo_steps, 1)
                pool.tensor_scalar(minus_mean_o[:], mv_o[:, :, 0], -1.0, None, ALU.mult).then_inc(rstdo_steps, 1)
                steps, left = settled(pool, 3 * n + 3), settled(pool, 16 * n)
                pool.wait_ge(setup_pool, 1)
                pool.wait_ge(rstdo_steps, steps)
                pool.wait_ge(stored, left)
                for b in range(B):
                    pool.tensor_scalar(fin[:, b], res[:, b], minus_mean_o[:, b:b + 1], rstd_o[:, b:b + 1],
                                       ALU.add, ALU.mult).then_inc(fin_made, 1)

            def step(i, c, j, after=True, now=True, two_before=True):
                if after:
                    cut_x(i + 1, (c + 1) % RING, 16 * (j + (c + 1) // RING + 1))
                if now:
                    add_skip(i, c % RING)
                    normalise_hidden(i, 0)
                    normalise_hidden(i, 1)
                if two_before:
                    normalise_out(i - 2)

            cut_x(0, 0, 16)
            for i in range(FIRST):
                step(i, i, 0, two_before=i >= 2)
            with pool.Fori(0, LOOPS) as j:
                for c in range(FIRST, FIRST + RING):
                    step(RING * j + c, c, j)
            for i in range(LAST, N + 2):
                step(i, i, 0, after=i + 1 < N, now=i < N)

        @block.scalar
        def _(act):
            act.dma_start(b1_all[:], b1.partition_broadcast(P)).then_inc(c_in, 16)
            for b in range(B):
                act.dma_start(b2_all[:, b], b2.partition_broadcast(P)).then_inc(c_in, 16)
            act.dma_start(gamma_col[:], gamma.rearrange("(b p) -> p b", p=P),
                          allow_slow_non_contiguous=True).then_inc(c_in, 16)
            act.dma_start(beta_col[:], beta.rearrange("(b p) -> p b", p=P),
                          allow_slow_non_contiguous=True).then_inc(c_in, 16)
            act.dma_start(row0_nat[:], adj[:, 0, :]).then_inc(c_in, 16)

            def cut_x(n, r, arrived):
                act.wait_ge(x_loaded[r], arrived)
                act.activation(x_hi[:], x_in[:, r], ACT.Copy).then_inc(xhi_made, 1)

            def keep_ht(n, r):
                act.wait_ge(ht_turned, n + 1)
                for b in range(B):
                    act.activation(HT[:, r, b], ht_ps[:, b], ACT.Copy,
                                   accum_out=counts[:, r, 0, b:b + 1]).then_inc(ht_made, 1)

            def cut_m(n, r):
                act.wait_ge(be_made, n + 1)
                act.wait_ge(m_done, n + 1)
                for b in range(B):
                    act.activation(m_hi[:, b], ma_ps[:, b], ACT.Copy,
                                   scale=recips[:, r, 0, b:b + 1]).then_inc(mhi_made, 1)

            def cut_a(n):
                act.wait_ge(a_done, n + 1)
                act.activation(a_hi[:], ma_ps[:], ACT.Copy).then_inc(ahi_made, 1)

            def relu(n, b):
                act.wait_ge(pre_made, B * n + b + 1)
                act.activation(act_h[:, b], pre[:, b], ACT.Relu).then_inc(relu_made, 1)

            def cut_t(n, b):
                act.wait_ge(t_turned, B * n + b + 1)
                act.activation(t_hi[:, b], t_ps[:, b], ACT.Copy).then_inc(thi_made, 1)

            def cut_y(n):
                act.wait_ge(y_done, n + 1)
                act.activation(y_hi[:], y_ps[:], ACT.Copy).then_inc(yhi_made, 1)

            def cut_p(n, r):
                act.wait_ge(p_done, n + 1)
                for b in range(B):
                    act.activation(p_hi[:, b], po_ps[:, b], ACT.Copy,
                                   scale=recips[:, r, 0, b:b + 1]).then_inc(phi_made, 1)

            def step(i, c, j, after=True, now=True, before=True, two_before=True):
                if two_before:
                    cut_p(i - 2, (c - 2) % RING)
                if after:
                    cut_x(i + 1, (c + 1) % RING, 16 * (j + (c + 1) // RING + 1))
                if now:
                    relu(i, 0)
                if after:
                    keep_ht(i + 1, (c + 1) % RING)
                if now:
                    relu(i, 1)
                if after:
                    cut_m(i + 1, (c + 1) % RING)
                if before:
                    cut_y(i - 1)
                if after:
                    cut_a(i + 1)
                if now:
                    cut_t(i, 0)
                    cut_t(i, 1)

            cut_x(0, 0, 16)
            for b in range(B):
                act.wait_ge(setup_pe, b + 1)
                act.activation(w1t_hi[:, b], z_ps[:, b], ACT.Copy).then_inc(setup_act, 1)
            act.wait_ge(c_in, 16 * C_LOADS)
            act.wait_ge(setup_dve, W2T_DONE)
            for b in range(HB):
                act.activation(w2g_hi[:, b], w2t[:, b], ACT.Copy,
                               scale=gamma_col[:, b:b + 1]).then_inc(setup_act, 1)
            keep_ht(0, 0)
            cut_m(0, 0)
            cut_a(0)
            for i in range(FIRST):
                step(i, i, 0, before=i >= 1, two_before=i >= 2)
            with act.Fori(0, LOOPS) as j:
                for c in range(FIRST, FIRST + RING):
                    step(RING * j + c, c, j)
            for i in range(LAST, N + 2):
                step(i, i, 0, after=i + 1 < N, now=i < N, before=i - 1 < N)

        @block.vector
        def _(dve):
            def make_h(n, r, arrived):
                dve.wait_ge(adj_loaded[r], arrived)
                dve.tensor_scalar(H[:, r], adj_in[:, r], 0.0, None, ALU.not_equal).then_inc(h_made, 1)

            def edge_scale(n, r):
                dve.wait_ge(ht_made, B * (n + 1))
                dve.tensor_scalar(clamp[:, 0], counts[:, r, 0], TINY, None, ALU.max).then_inc(be_clamped, 1)
                dve.wait_ge(be_clamped, n + 1)
                dve.reciprocal(recips[:, r, 0], clamp[:, 0]).then_inc(be_made, 1)

            def node_scale(n, r):
                dve.wait_ge(deg_done, n + 1)
                dve.tensor_reduce(counts[:, r, 1], ht_ps[:, :, 0:2], AX.X, ALU.add).then_inc(deg_summed, 1)
                dve.wait_ge(deg_summed, n + 1)
                dve.tensor_scalar(clamp[:, 1], counts[:, r, 1], TINY, None, ALU.max).then_inc(deg_clamped, 1)
                dve.wait_ge(deg_clamped, n + 1)
                dve.reciprocal(recips[:, r, 1], clamp[:, 1]).then_inc(deg_inverted, 1)
                dve.wait_ge(deg_inverted, n + 1)
                dve.scalar_tensor_tensor(out=dn[:, r], in0=counts[:, r, 1], scalar=0.0, in1=recips[:, r, 1],
                                         op0=ALU.is_gt, op1=ALU.mult).then_inc(dn_made, 1)

            def cut_m(n, r):
                dve.wait_ge(mhi_made, B * (n + 1))
                for b in range(B):
                    dve.scalar_tensor_tensor(out=m_lo[:, b], in0=ma_ps[:, b], scalar=recips[:, r, 0, b:b + 1],
                                             in1=read(m_hi[:, b]), op0=ALU.mult,
                                             op1=ALU.subtract).then_inc(mlo_made, 1)

            def cut_a(n):
                dve.wait_ge(ahi_made, n + 1)
                dve.tensor_tensor(a_lo[:], ma_ps[:], read(a_hi[:]), ALU.subtract).then_inc(alo_made, 1)

            def scale_z(n, r, b):
                dve.wait_ge(dn_made, n + 1)
                dve.wait_ge(z_done, B * n + b + 1)
                dve.scalar_tensor_tensor(out=pre[:, b], in0=z_ps[:, b], scalar=dn[:, r, b:b + 1],
                                         in1=b1_all[:], op0=ALU.mult, op1=ALU.add).then_inc(pre_made, 1)

            def hidden_stats(n, b):
                dve.wait_ge(relu_made, B * n + b + 1)
                dve.bn_stats(bn_h[:, b], act_h[:, b]).then_inc(bnh_made, 1)

            def hidden_moments(n, b):
                k = settled(dve, B * n + b + 1)
                dve.wait_ge(setup_dve, 1)
                dve.wait_ge(bnh_made, k)
                dve.bn_aggr(mv_h[:, b], bn_h[:, b]).then_inc(mvh_made, 1)

            def cut_t(n, b):
                dve.wait_ge(thi_made, B * n + b + 1)
                dve.tensor_tensor(t_lo[:, b], t_ps[:, b], read(t_hi[:, b]), ALU.subtract).then_inc(tlo_made, 1)

            def cut_y(n):
                dve.wait_ge(yhi_made, n + 1)
                dve.tensor_tensor(y_lo[:], y_ps[:], read(y_hi[:]), ALU.subtract).then_inc(ylo_made, 1)

            def cut_p(n, r):
                dve.wait_ge(phi_made, B * (n + 1))
                for b in range(B):
                    dve.scalar_tensor_tensor(out=p_lo[:, b], in0=po_ps[:, b], scalar=recips[:, r, 0, b:b + 1],
                                             in1=read(p_hi[:, b]), op0=ALU.mult,
                                             op1=ALU.subtract).then_inc(plo_made, 1)

            def add_up(n, r, reused):
                dve.wait_ge(o_done, n + 1)
                dve.wait_ge(skip_made, n + 1)
                if reused:
                    dve.wait_ge(fin_made, B * n)
                for b in range(B):
                    dve.scalar_tensor_tensor(out=res[:, b], in0=po_ps[:, b], scalar=dn[:, r, b:b + 1],
                                             in1=skip[:, r, b], op0=ALU.mult, op1=ALU.add).then_inc(res_made, 1)

            def out_moments(n):
                for b in range(B):
                    dve.wait_ge(res_made, B * n + b + 1)
                    dve.bn_stats(bn_o[:, b], res[:, b]).then_inc(bno_made, 1)
                k = settled(dve, B * (n + 1))
                dve.wait_ge(setup_dve, 1)
                dve.wait_ge(bno_made, k)
                for b in range(B):
                    dve.bn_aggr(mv_o[:, b], bn_o[:, b]).then_inc(mvo_made, 1)

            def step(i, c, j, after=True, now=True, before=True, two_before=True):
                if after:
                    make_h(i + 1, (c + 1) % RING, 16 * (j + (c + 1) // RING + 1))
                if two_before:
                    cut_p(i - 2, (c - 2) % RING)
                if now:
                    scale_z(i, c % RING, 0)
                    scale_z(i, c % RING, 1)
                    hidden_stats(i, 0)
                if after:
                    edge_scale(i + 1, (c + 1) % RING)
                if now:
                    hidden_moments(i, 0)
                    hidden_stats(i, 1)
                if two_before:
                    add_up(i - 2, (c - 2) % RING, not isinstance(i, int) or i > 2)
                if now:
                    hidden_moments(i, 1)
                if after:
                    node_scale(i + 1, (c + 1) % RING)
                    cut_m(i + 1, (c + 1) % RING)
                if two_before:
                    out_moments(i - 2)
                if before:
                    cut_y(i - 1)
                if after:
                    cut_a(i + 1)
                if now:
                    cut_t(i, 0)
                    cut_t(i, 1)

            make_h(0, 0, 16)
            for b in range(B):
                dve.wait_ge(setup_act, b + 1)
                dve.tensor_tensor(w1t_lo[:, b], z_ps[:, b], read(w1t_hi[:, b]), ALU.subtract).then_inc(setup_dve, 1)
            for b in range(B):
                dve.wait_ge(setup_pe, B + b + 1)
                dve.tensor_copy(w2t[:, :, b * P:(b + 1) * P], t_ps[:, b]).then_inc(setup_dve, 1)
            dve.wait_ge(setup_pe, 2 * B + 1)
            for b in range(B):
                turned = ht_ps[:, b, 0:N]
                dve.tensor_copy(row0_cut[:, b, :, 0], turned).then_inc(row0_steps, 1)
                dve.wait_ge(row0_steps, 2 * b + 1)
                dve.tensor_tensor(row0_cut[:, b, :, 1], turned, read(row0_cut[:, b, :, 0]),
                                  ALU.subtract).then_inc(row0_steps, 1)
            dve.wait_ge(c_in, 16 * C_LOADS)
            dve.wait_ge(setup_pool, 2)
            for b in range(HB):
                dve.tensor_scalar(beta_wide[:, b], ones[:], beta_col[:, b:b + 1], None, ALU.mult).then_inc(setup_dve, 1)
            dve.tensor_scalar(averager[:], ones[:], 2.0 / P, None, ALU.mult).then_inc(setup_dve, 1)
            for b in range(HB):
                dve.wait_ge(setup_act, B + b + 1)
                dve.scalar_tensor_tensor(out=w2g_lo[:, b], in0=w2t[:, b], scalar=gamma_col[:, b:b + 1],
                                         in1=read(w2g_hi[:, b]), op0=ALU.mult,
                                         op1=ALU.subtract).then_inc(setup_dve, 1)
            dve.wait_ge(setup_pe, 2 * B + 2)
            dve.tensor_copy(bias_rows[:], y_ps[:, 0]).then_inc(bias_steps, 1)
            dve.wait_ge(bias_steps, 1)
            dve.tensor_tensor(bias_rows[P // 2:P], y_ps[P // 2:P, 0], read(bias_rows[P // 2:P]),
                              ALU.subtract).then_inc(bias_steps, 1)
            edge_scale(0, 0)
            node_scale(0, 0)
            cut_m(0, 0)
            cut_a(0)
            for i in range(FIRST):
                step(i, i, 0, before=i >= 1, two_before=i >= 2)
            with dve.Fori(0, LOOPS) as j:
                for c in range(FIRST, FIRST + RING):
                    step(RING * j + c, c, j)
            for i in range(LAST, N + 2):
                step(i, i, 0, after=i + 1 < N, now=i < N, before=i - 1 < N)

        @block.tensor
        def _(pe):
            def product(out, pairs, start=True, stop=True):
                for k, (lhs, rhs) in enumerate(pairs):
                    mm = pe.matmul(out, lhs, rhs, start=start and k == 0, stop=stop and k == len(pairs) - 1)
                return mm

            def turn_h(n, r, reused):
                pe.wait_ge(h_made, n + 1)
                if reused:
                    pe.wait_ge(deg_summed, n)
                for e in range(B):
                    for b in range(B):
                        mm = pe.transpose(ht_ps[:, e, b * P:(b + 1) * P], read(H[:, r, b, e * P:(e + 1) * P]),
                                          ident[:])
                mm.then_inc(ht_turned, 1)

            def edge_sums(n, r):
                pe.wait_ge(xhi_made, n + 1)
                pe.wait_ge(xlo_made, n + 1)
                for e in range(B):
                    mm = product(ma_ps[:, e], [(H[:, r, b, e * P:(e + 1) * P], part[:, b])
                                               for part in (x_hi, x_lo) for b in range(B)])
                mm.then_inc(m_done, 1)

            def degrees(n, r):
                pe.wait_ge(ht_made, B * (n + 1))
                for b in range(B):
                    mm = product(ht_ps[:, b, 0:2], [(HT[:, r, e, b * P:(b + 1) * P], row0_cut[:, e, n, :])
                                                    for e in range(B)])
                mm.then_inc(deg_done, 1)

            def node_sums(n, r):
                pe.wait_ge(mhi_made, B * (n + 1))
                pe.wait_ge(mlo_made, B * (n + 1))
                for d in range(B):
                    mm = product(ma_ps[:, d], [(part[:, e, d * P:(d + 1) * P], HT[:, r, e])
                                               for part in (m_hi, m_lo) for e in range(B)])
                mm.then_inc(a_done, 1)

            def hidden(n, reused):
                pe.wait_ge(ahi_made, n + 1)
                pe.wait_ge(alo_made, n + 1)
                for b in range(B):
                    if reused:
                        pe.wait_ge(pre_made, B * n + b - 1)
                    mm = product(z_ps[:, b], [(a[:, d, b * P:(b + 1) * P], w[:, d])
                                              for a, w in ((a_hi, w1t_hi), (a_hi, w1t_lo), (a_lo, w1t_hi))
                                              for d in range(B)])
                    mm.then_inc(z_done, 1)

            def turn_t(n, b):
                pe.wait_ge(norm_made, B * n + b + 1)
                for h in range(HB):
                    mm = pe.transpose(t_ps[:, b, h], norm_h[:, b, h * P:(h + 1) * P], ident[:])
                mm.then_inc(t_turned, 1)

            def project(n):
                for b in range(B):
                    pe.wait_ge(thi_made, B * n + b + 1)
                    pe.matmul(y_ps[:, b], averager[:], bias_rows[:], start=True, stop=False)
                    product(y_ps[:, b], [(t_hi[:, b, h], w[:, h]) for w in (w2g_hi, w2g_lo) for h in range(HB)],
                            start=False, stop=False)
                    pe.wait_ge(tlo_made, B * n + b + 1)
                    mm = product(y_ps[:, b], [(t_lo[:, b, h], w2g_hi[:, h]) for h in range(HB)], start=False)
                mm.then_inc(y_done, 1)

            def edge_sums_2(n, r, reused):
                pe.wait_ge(yhi_made, n + 1)
                pe.wait_ge(ylo_made, n + 1)
                if reused:
                    pe.wait_ge(res_made, B * n)
                for e in range(B):
                    mm = product(po_ps[:, e], [(H[:, r, b, e * P:(e + 1) * P], part[:, b])
                                               for part in (y_hi, y_lo) for b in range(B)])
                mm.then_inc(p_done, 1)

            def node_sums_2(n, r):
                pe.wait_ge(phi_made, B * (n + 1))
                pe.wait_ge(plo_made, B * (n + 1))
                for b in range(B):
                    mm = product(po_ps[:, b], [(HT[:, r, e, b * P:(b + 1) * P], part[:, e])
                                               for part in (p_hi, p_lo) for e in range(B)])
                mm.then_inc(o_done, 1)

            def step(i, c, after=True, now=True, before=True, two_before=True):
                peeled = isinstance(i, int)
                if now:
                    hidden(i, not peeled or i > 0)
                if after:
                    turn_h(i + 1, (c + 1) % RING, True)
                if two_before:
                    node_sums_2(i - 2, (c - 2) % RING)
                if after:
                    edge_sums(i + 1, (c + 1) % RING)
                    degrees(i + 1, (c + 1) % RING)
                if before:
                    project(i - 1)
                if after:
                    node_sums(i + 1, (c + 1) % RING)
                if now:
                    turn_t(i, 0)
                    turn_t(i, 1)
                if before:
                    edge_sums_2(i - 1, (c - 1) % RING, not peeled or i > 1)

            pe.wait_ge(w_in, 32)
            pe.wait_ge(setup_pool, 4)
            for b in range(B):
                for h in range(HB):
                    mm = pe.transpose(z_ps[:, b, h * P:(h + 1) * P], w1_nat[:, h, b * P:(b + 1) * P], ident[:])
                mm.then_inc(setup_pe, 1)
            for b in range(B):
                for h in range(HB):
                    mm = pe.transpose(t_ps[:, b, h], w2_nat[:, b, h * P:(h + 1) * P], ident[:])
                mm.then_inc(setup_pe, 1)
            pe.wait_ge(c_in, 16 * C_LOADS)
            for b in range(B):
                mm = pe.transpose(ht_ps[:, b, 0:N], row0_nat[:, b * P:(b + 1) * P], ident[0:N, 0:N])
            mm.then_inc(setup_pe, 1)
            pe.wait_ge(setup_dve, W2T_DONE + HB + 1)
            mm = product(y_ps[:, 0], [(beta_wide[:, h], w2t[:, h]) for h in range(HB)])
            mm.then_inc(setup_pe, 1)

            pe.wait_ge(row0_steps, 2 * B)
            turn_h(0, 0, False)
            edge_sums(0, 0)
            degrees(0, 0)
            node_sums(0, 0)
            pe.wait_ge(setup_dve, W2T_DONE + 2 * HB + 1)
            pe.wait_ge(bias_steps, 2)
            for i in range(FIRST):
                step(i, i, before=i >= 1, two_before=i >= 2)
            with pe.Fori(0, LOOPS) as j:
                for c in range(FIRST, FIRST + RING):
                    step(RING * j + c, c)
            for i in range(LAST, N + 2):
                step(i, i, after=i + 1 < N, now=i < N, before=i - 1 < N)


_INS = ["x", "adj", "L0_gnn_W1", "L0_gnn_b1", "L0_gnn_gamma", "L0_gnn_beta", "L0_gnn_W2", "L0_gnn_b2"]


def kernel(**inputs):
    import numpy as _np
    import concourse.bacc as _bacc
    from concourse import mybir as _mybir
    from concourse.bass_utils import run_bass_kernel_spmd as _run

    nc = _bacc.Bacc("TRN2", target_bir_lowering=False, num_devices=1)
    arrays, args = {}, []
    for name in _INS:
        a = _np.ascontiguousarray(inputs[name])
        arrays[f"in_{name}"] = a
        args.append(nc.dram_tensor(f"in_{name}", a.shape, _mybir.dt.from_np(a.dtype), kind="ExternalInput").ap())
    shape = arrays["in_x"].shape
    out = nc.dram_tensor("out_0", shape, _mybir.dt.float32, kind="ExternalOutput").ap()
    hypergraph_kernel(nc, *args, out)
    r = _run(nc, [arrays], core_ids=[0])
    return r.results[0]["out_0"]
```

```python
import concourse.bass as bass
from concourse import mybir
from contextlib import ExitStack


def hypergraph_kernel(nc, x, adj, w1, b1, gamma, beta, w2, b2, out):
    f32 = mybir.dt.float32
    f32r = mybir.dt.float32r
    bf16 = mybir.dt.bfloat16
    ALU = mybir.AluOpType
    ACT = mybir.ActivationFunctionType
    AX = mybir.AxisListType

    P = nc.NUM_PARTITIONS
    N, C, D = x.shape
    DH = w1.shape[0]
    B = C // P
    HB = DH // P
    EPS = 1e-5
    PARTS = 3
    TINY = 1.2e-38
    RING = 4
    FIRST = 5
    LOOPS = (N - FIRST) // RING
    LAST = FIRST + RING * LOOPS
    assert (B, HB) == (2, 4) and N % RING == 0 and LAST == N - 3

    x_rows = x.rearrange("n (p b) d -> n p b d", b=B)
    adj_rows = adj.rearrange("n (p b) e -> n p b e", b=B)
    out_rows = out.rearrange("n (p b) d -> n p b d", b=B)

    ctx = ExitStack()
    with ctx:
        def sb(name, shape, dt=f32):
            return ctx.enter_context(nc.sbuf_tensor(name, shape, dt))

        def ps(name, shape):
            return ctx.enter_context(nc.psum_tensor(name, shape, f32))

        def sem(name):
            return ctx.enter_context(nc.semaphore(name))

        ident = sb("ident", [P, P])
        ident_16 = sb("ident_16", [P, P], bf16)
        w1_nat = sb("w1_nat", [P, HB, D])
        w2_nat = sb("w2_nat", [P, B, DH])
        w1t_hi = sb("w1t_hi", [P, B, DH], f32r)
        w1t_lo = sb("w1t_lo", [P, B, DH], f32r)
        w2t = sb("w2t", [P, HB, D])
        w2g_hi = sb("w2g_hi", [P, HB, D], f32r)
        w2g_lo = sb("w2g_lo", [P, HB, D], f32r)
        gamma_col = sb("gamma_col", [P, HB])
        beta_col = sb("beta_col", [P, HB])
        beta_wide = sb("beta_wide", [P, HB, P])
        ones = sb("ones", [P, P])
        b1_all = sb("b1_all", [P, DH])
        b2_all = sb("b2_all", [P, B, D])
        beta_w2 = sb("beta_w2", [P, B, D])
        row0_nat = sb("row0_nat", [N, C])
        row0_rest = sb("row0_rest", [P, B, 2, N])
        row0_cut = sb("row0_cut", [P, B, N, PARTS], bf16)
        row0_now = sb("row0_now", [P, RING, B, PARTS], bf16)
        minus_half = sb("minus_half", [P, B])

        adj_in = sb("adj_in", [P, RING, B, C])
        x_in = sb("x_in", [P, RING, B, D])
        H = sb("H", [P, RING, B, C], f32r)
        H16 = sb("H16", [P, B, C], bf16)
        HT16 = sb("HT16", [P, B, C], bf16)
        HT = sb("HT", [P, RING, B, C], f32r)
        skip = sb("skip", [P, RING, B, D])
        counts = sb("counts", [P, RING, 2, B])
        recips = sb("recips", [P, RING, 2, B])
        dn = sb("dn", [P, RING, B])
        clamp = sb("clamp", [P, 2, B])
        x_hi = sb("x_hi", [P, B, D], f32r)
        x_lo = sb("x_lo", [P, B, D], f32r)
        m_hi = sb("m_hi", [P, B, D], f32r)
        m_lo = sb("m_lo", [P, B, D], f32r)
        a_hi = sb("a_hi", [P, B, C], f32r)
        a_lo = sb("a_lo", [P, B, C], f32r)
        pre = sb("pre", [P, B, DH])
        act_h = sb("act_h", [P, B, DH])
        norm_h = sb("norm_h", [P, B, DH])
        bn_h = sb("bn_h", [P, B, 6])
        mv_h = sb("mv_h", [P, B, 2])
        var_h = sb("var_h", [P, B])
        rstd_h = sb("rstd_h", [P, B])
        minus_mean_h = sb("minus_mean_h", [P, B])
        t_hi = sb("t_hi", [P, B, HB, P], f32r)
        t_lo = sb("t_lo", [P, B, HB, P], f32r)
        y_sum = sb("y_sum", [P, B, D])
        y_hi = sb("y_hi", [P, B, D], f32r)
        y_lo = sb("y_lo", [P, B, D], f32r)
        p_hi = sb("p_hi", [P, B, D], f32r)
        p_lo = sb("p_lo", [P, B, D], f32r)
        res = sb("res", [P, 2, B, D])
        bn_o = sb("bn_o", [P, 2, B, 6])
        mv_o = sb("mv_o", [P, 2, B, 2])
        var_o = sb("var_o", [P, 2, B])
        rstd_o = sb("rstd_o", [P, 2, B])
        minus_mean_o = sb("minus_mean_o", [P, 2, B])
        shift_o = sb("shift_o", [P, 2, B])
        fin = sb("fin", [P, 2, B, D])

        ht_ps = ps("ht_ps", [P, B, C])
        ma_ps = ps("ma_ps", [P, B, C])
        y_ps = ps("y_ps", [P, B, D])
        po_ps = ps("po_ps", [P, B, D])
        z_ps = ps("z_ps", [P, B, DH])
        t_ps = ps("t_ps", [P, B, HB, P])
        last_po_ps, last_p_hi, last_p_lo = z_ps[:, :, 0:D], x_hi, x_lo

        w1_in = sem("w1_in")
        w2_in = sem("w2_in")
        row0_in = sem("row0_in")
        b1_in = sem("b1_in")
        scales_in = sem("scales_in")
        b2_in = sem("b2_in")
        setup_pool = sem("setup_pool")
        ident_made = sem("ident_made")
        w1_turned = sem("w1_turned")
        w1hi_made = sem("w1hi_made")
        w1lo_made = sem("w1lo_made")
        row0_turned = sem("row0_turned")
        row0_steps = sem("row0_steps")
        w2_turned = sem("w2_turned")
        w2_kept = sem("w2_kept")
        w2hi_made = sem("w2hi_made")
        w2lo_made = sem("w2lo_made")
        beta_spread = sem("beta_spread")
        bias_done = sem("bias_done")
        bias_kept = sem("bias_kept")
        adj_loaded = [sem(f"adj_loaded{r}") for r in range(RING)]
        x_loaded = [sem(f"x_loaded{r}") for r in range(RING)]
        h_made = sem("h_made")
        xhi_made = sem("xhi_made")
        xlo_made = sem("xlo_made")
        h16_made = sem("h16_made")
        ht16_made = sem("ht16_made")
        doubled = sem("doubled")
        skip_made = sem("skip_made")
        row0_copied = sem("row0_copied")
        ht_turned = sem("ht_turned")
        ht_made = sem("ht_made")
        m_done = sem("m_done")
        deg_done = sem("deg_done")
        deg_summed = sem("deg_summed")
        be_clamped = sem("be_clamped")
        be_made = sem("be_made")
        deg_clamped = sem("deg_clamped")
        deg_inverted = sem("deg_inverted")
        dn_made = sem("dn_made")
        mhi_made = sem("mhi_made")
        mlo_made = sem("mlo_made")
        a_done = sem("a_done")
        ahi_made = sem("ahi_made")
        alo_made = sem("alo_made")
        z_done = sem("z_done")
        pre_made = sem("pre_made")
        relu_made = sem("relu_made")
        bnh_made = sem("bnh_made")
        mvh_made = sem("mvh_made")
        rstdh_steps = sem("rstdh_steps")
        norm_made = sem("norm_made")
        t_turned = sem("t_turned")
        thi_made = sem("thi_made")
        tlo_made = sem("tlo_made")
        y_done = sem("y_done")
        ysum_made = sem("ysum_made")
        yhi_made = sem("yhi_made")
        ylo_made = sem("ylo_made")
        p_done = sem("p_done")
        phi_made = sem("phi_made")
        plo_made = sem("plo_made")
        o_done = sem("o_done")
        res_made = sem("res_made")
        bno_made = sem("bno_made")
        mvo_made = sem("mvo_made")
        rstdo_steps = sem("rstdo_steps")
        fin_made = sem("fin_made")
        stored = [sem("stored_even"), sem("stored_odd")]

        def settled(engine, value):
            return value if isinstance(value, int) else engine.to_reg(value)

        def read(cut):
            return cut.bitcast(f32)

        block = ctx.enter_context(nc.Block())

        @block.sync
        def _(sp):
            def load(n, r, again):
                if again:
                    sp.wait_ge(h_made, n - RING + 1)
                sp.dma_start(adj_in[:, r], adj_rows[n]).then_inc(adj_loaded[r], 16)
                if again:
                    sp.wait_ge(xhi_made, n - RING + 1)
                    sp.wait_ge(xlo_made, n - RING + 1)
                    sp.wait_ge(doubled, n - RING + 1)
                sp.dma_start(x_in[:, r], x_rows[n]).then_inc(x_loaded[r], 16)

            def store(n, q):
                sp.wait_ge(fin_made, 2 * (n + 1))
                sp.dma_start(out_rows[n], fin[:, q]).then_inc(stored[q], 16)

            load(0, 0, False)
            sp.dma_start(row0_nat[:], adj[:, 0, :]).then_inc(row0_in, 16)
            sp.dma_start(w1_nat[:], w1.rearrange("(b p) d -> p b d", p=P)).then_inc(w1_in, 16)
            load(1, 1, False)
            sp.dma_start(b1_all[:], b1.partition_broadcast(P)).then_inc(b1_in, 16)
            sp.dma_start(w2_nat[:], w2.rearrange("(b p) h -> p b h", p=P)).then_inc(w2_in, 16)
            sp.dma_start(gamma_col[:], gamma.rearrange("(b p) -> p b", p=P),
                         allow_slow_non_contiguous=True).then_inc(scales_in, 16)
            sp.dma_start(beta_col[:], beta.rearrange("(b p) -> p b", p=P),
                         allow_slow_non_contiguous=True).then_inc(scales_in, 16)
            for b in range(B):
                sp.dma_start(b2_all[:, b], b2.partition_broadcast(P)).then_inc(b2_in, 16)
            for n in range(2, RING):
                load(n, n, False)
            for n in range(RING, 2 * RING):
                load(n, n - RING, True)
                if n > RING:
                    store(n - RING - 1, (n - RING - 1) % 2)
            with sp.Fori(2, N // RING) as j:
                for c in range(RING):
                    load(RING * j + c, c, True)
                    store(RING * j + c - RING - 1, (c - 1) % 2)
            for n in range(N - RING - 1, N):
                store(n, n % 2)
            for q in range(2):
                sp.wait_ge(stored[q], 16 * N // 2)

        @block.gpsimd
        def _(pool):
            pool.memset(ident[:], 0.0).then_inc(setup_pool, 1)
            pool.memset(ones[:], 1.0).then_inc(setup_pool, 1)
            pool.memset(minus_half[:], -0.5).then_inc(setup_pool, 1)
            pool.wait_ge(setup_pool, 3)
            pool.affine_select(out=ident[:], in_=ident[:], compare_op=ALU.not_equal, fill=1.0, base=0,
                               pattern=[[-1, P]], channel_multiplier=1).then_inc(setup_pool, 1)

            def cut_x(n, r, arrived):
                pool.wait_ge(x_loaded[r], arrived)
                pool.wait_ge(xhi_made, n + 1)
                pool.tensor_tensor(x_lo[:], x_in[:, r], read(x_hi[:]), ALU.subtract).then_inc(xlo_made, 1)

            def add_skip(n, r):
                pool.wait_ge(doubled, n + 1)
                pool.tensor_tensor(skip[:, r], skip[:, r], b2_all[:], ALU.add).then_inc(skip_made, 1)

            def cut_y(n):
                pool.wait_ge(yhi_made, n + 1)
                pool.tensor_tensor(y_lo[:], y_sum[:], read(y_hi[:]), ALU.subtract).then_inc(ylo_made, 1)

            def normalise_hidden(n, b):
                k = B * n + b
                made = settled(pool, k + 1)
                pool.wait_ge(setup_pool, 1)
                pool.wait_ge(mvh_made, made)
                pool.tensor_scalar(var_h[:, b:b + 1], mv_h[:, b, 1:2], EPS, None, ALU.add).then_inc(rstdh_steps, 1)
                pool.wait_ge(rstdh_steps, 3 * k + 1)
                pool.tensor_tensor(rstd_h[:, b:b + 1], var_h[:, b:b + 1], minus_half[:, 0:1],
                                   ALU.pow).then_inc(rstdh_steps, 1)
                pool.tensor_scalar(minus_mean_h[:, b:b + 1], mv_h[:, b, 0:1], -1.0, None,
                                   ALU.mult).then_inc(rstdh_steps, 1)
                steps = settled(pool, 3 * k + 3)
                pool.wait_ge(setup_pool, 1)
                pool.wait_ge(rstdh_steps, steps)
                pool.tensor_scalar(norm_h[:, b], act_h[:, b], minus_mean_h[:, b:b + 1], rstd_h[:, b:b + 1],
                                   ALU.add, ALU.mult).then_inc(norm_made, 1)

            def out_scale(n, q):
                made = settled(pool, B * (n + 1))
                pool.wait_ge(setup_pool, 1)
                pool.wait_ge(mvo_made, made)
                pool.tensor_scalar(var_o[:, q], mv_o[:, q, :, 1], EPS, None, ALU.add).then_inc(rstdo_steps, 1)
                pool.wait_ge(rstdo_steps, 4 * n + 1)
                pool.tensor_tensor(rstd_o[:, q], var_o[:, q], minus_half[:], ALU.pow).then_inc(rstdo_steps, 1)
                pool.tensor_scalar(minus_mean_o[:, q], mv_o[:, q, :, 0], -1.0, None, ALU.mult).then_inc(rstdo_steps, 1)
                pool.wait_ge(rstdo_steps, 4 * n + 3)
                pool.tensor_tensor(shift_o[:, q], minus_mean_o[:, q], rstd_o[:, q], ALU.mult).then_inc(rstdo_steps, 1)

            def step(i, c, j, two_after=True, after=True, before=True, three_before=True):
                if three_before:
                    out_scale(i - 3, (c - 3) % 2)
                if after:
                    add_skip(i, c % RING)
                normalise_hidden(i, 0)
                normalise_hidden(i, 1)
                if before:
                    cut_y(i - 1)
                if not after:
                    add_skip(i, c % RING)
                if two_after:
                    cut_x(i + 2, (c + 2) % RING, 16 * (j + (c + 2) // RING + 1))

            cut_x(1, 1, 16)
            pool.wait_ge(b2_in, 16 * B)
            for i in range(FIRST):
                step(i, i, 0, before=i >= 1, three_before=i >= 3)
            with pool.Fori(0, LOOPS) as j:
                for c in range(FIRST, FIRST + RING):
                    step(RING * j + c, c, j)
            for i in range(LAST, N):
                step(i, i, 0, two_after=i + 2 < N, after=i + 1 < N)
            for n in range(N - 3, N):
                out_scale(n, n % 2)

        @block.scalar
        def _(act):
            def cut_x(n, r, arrived):
                act.wait_ge(x_loaded[r], arrived)
                act.activation(x_hi[:], x_in[:, r], ACT.Copy).then_inc(xhi_made, 1)

            def keep_ht(n, r):
                act.wait_ge(ht_turned, n + 1)
                for b in range(B):
                    act.activation(HT[:, r, b], ht_ps[:, b], ACT.Copy,
                                   accum_out=counts[:, r, 0, b:b + 1]).then_inc(ht_made, 1)

            def pick_row0(n, r):
                act.activation(row0_now[:, r], row0_cut[:, :, n, :], ACT.Copy).then_inc(row0_copied, 1)

            def double(n, r):
                act.activation(skip[:, r], x_in[:, r], ACT.Copy, scale=2.0).then_inc(doubled, 1)

            def copy_h(n, r):
                act.wait_ge(h_made, n + 1)
                act.activation(H16[:], read(H[:, r]), ACT.Copy).then_inc(h16_made, 1)

            def copy_ht(n):
                act.activation(HT16[:], ht_ps[:], ACT.Copy).then_inc(ht16_made, 1)

            def normalise_out(n, q, b, pair):
                act.wait_ge(rstdo_steps, 4 * (n + 1))
                if not isinstance(n, int) or n > 1:
                    act.wait_ge(stored[q], 16 * pair)
                act.activation(fin[:, q, b], res[:, q, b], ACT.Identity, bias=shift_o[:, q, b:b + 1],
                               scale=rstd_o[:, q, b:b + 1]).then_inc(fin_made, 1)

            def cut_m(n, r):
                act.wait_ge(be_made, n + 1)
                act.wait_ge(m_done, n + 1)
                for b in range(B):
                    act.activation(m_hi[:, b], ma_ps[:, b], ACT.Copy,
                                   scale=recips[:, r, 0, b:b + 1]).then_inc(mhi_made, 1)

            def cut_a(n):
                act.wait_ge(a_done, n + 1)
                act.activation(a_hi[:], ma_ps[:], ACT.Copy).then_inc(ahi_made, 1)

            def relu(n, b):
                act.wait_ge(pre_made, B * n + b + 1)
                act.activation(act_h[:, b], pre[:, b], ACT.Relu).then_inc(relu_made, 1)

            def cut_t(n, b):
                act.wait_ge(t_turned, B * n + b + 1)
                act.activation(t_hi[:, b], t_ps[:, b], ACT.Copy).then_inc(thi_made, 1)

            def cut_y(n):
                act.wait_ge(ysum_made, n + 1)
                act.activation(y_hi[:], y_sum[:], ACT.Copy).then_inc(yhi_made, 1)

            def cut_p(n, r, p, hi):
                act.wait_ge(p_done, n + 1)
                for b in range(B):
                    act.activation(hi[:, b], p[:, b], ACT.Copy,
                                   scale=recips[:, r, 0, b:b + 1]).then_inc(phi_made, 1)

            def cut_w2():
                act.wait_ge(scales_in, 32)
                act.wait_ge(w2_kept, B)
                for b in range(HB):
                    act.activation(w2g_hi[:, b], w2t[:, b], ACT.Copy,
                                   scale=gamma_col[:, b:b + 1]).then_inc(w2hi_made, 1)

            def step(i, c, j, two_after=True, after=True, before=True, two_before=True, three_before=True,
                     setup=False):
                this, behind, ahead, far = c % RING, (c - 2) % RING, (c + 1) % RING, (c + 2) % RING
                double(i, this)
                if after:
                    copy_h(i + 1, ahead)
                relu(i, 0)
                if after:
                    keep_ht(i + 1, ahead)
                relu(i, 1)
                if after:
                    cut_m(i + 1, ahead)
                if two_before:
                    cut_p(i - 2, behind, po_ps, p_hi)
                if after:
                    pick_row0(i + 1, ahead)
                    copy_ht(i + 1)
                if three_before:
                    normalise_out(i - 3, (c - 3) % 2, 0, RING // 2 * j + (c - 3) // 2)
                if after:
                    cut_a(i + 1)
                if setup:
                    cut_w2()
                if three_before:
                    normalise_out(i - 3, (c - 3) % 2, 1, RING // 2 * j + (c - 3) // 2)
                if before:
                    cut_y(i - 1)
                cut_t(i, 0)
                cut_t(i, 1)
                if two_after:
                    cut_x(i + 2, far, 16 * (j + (c + 2) // RING + 1))

            copy_h(0, 0)
            cut_x(0, 0, 16)
            keep_ht(0, 0)
            copy_ht(0)
            cut_m(0, 0)
            for b in range(B):
                act.wait_ge(w1_turned, b + 1)
                act.activation(w1t_hi[:, b], z_ps[:, b], ACT.Copy).then_inc(w1hi_made, 1)
            act.wait_ge(row0_steps, 5)
            pick_row0(0, 0)
            cut_a(0)
            cut_x(1, 1, 16)
            step(0, 0, 0, before=False, two_before=False, three_before=False, setup=True)
            for i in range(1, FIRST):
                step(i, i, 0, two_before=i >= 2, three_before=i >= 3)
            with act.Fori(0, LOOPS) as j:
                for c in range(FIRST, FIRST + RING):
                    step(RING * j + c, c, j)
            for i in range(LAST, N):
                step(i, i, 0, two_after=i + 2 < N, after=i + 1 < N)
            act.wait_ge(p_done, N - 1)
            cut_y(N - 1)
            cut_p(N - 2, (N - 2) % RING, po_ps, p_hi)
            for b in range(B):
                normalise_out(N - 3, (N - 3) % 2, b, (N - 3) // 2)
            cut_p(N - 1, (N - 1) % RING, last_po_ps, last_p_hi)
            for n in range(N - 2, N):
                for b in range(B):
                    normalise_out(n, n % 2, b, n // 2)

        @block.vector
        def _(dve):
            def make_h(n, r, arrived):
                dve.wait_ge(adj_loaded[r], arrived)
                dve.tensor_scalar(H[:, r], adj_in[:, r], 0.0, None, ALU.not_equal).then_inc(h_made, 1)

            def clamp_counts(n, r):
                dve.wait_ge(ht_made, B * (n + 1))
                dve.tensor_scalar(clamp[:, 0], counts[:, r, 0], TINY, None, ALU.max).then_inc(be_clamped, 1)

            def invert_counts(n, r):
                dve.wait_ge(be_clamped, n + 1)
                dve.reciprocal(recips[:, r, 0], clamp[:, 0]).then_inc(be_made, 1)

            def sum_degrees(n, r):
                dve.wait_ge(deg_done, n + 1)
                dve.tensor_reduce(counts[:, r, 1], ht_ps[:, :, 0:PARTS], AX.X, ALU.add).then_inc(deg_summed, 1)

            def clamp_degrees(n, r):
                dve.wait_ge(deg_summed, n + 1)
                dve.tensor_scalar(clamp[:, 1], counts[:, r, 1], TINY, None, ALU.max).then_inc(deg_clamped, 1)

            def invert_degrees(n, r):
                dve.wait_ge(deg_clamped, n + 1)
                dve.reciprocal(recips[:, r, 1], clamp[:, 1]).then_inc(deg_inverted, 1)

            def node_scale(n, r):
                dve.wait_ge(deg_inverted, n + 1)
                dve.scalar_tensor_tensor(out=dn[:, r], in0=counts[:, r, 1], scalar=0.0, in1=recips[:, r, 1],
                                         op0=ALU.is_gt, op1=ALU.mult).then_inc(dn_made, 1)

            def cut_m(n, r):
                dve.wait_ge(mhi_made, B * (n + 1))
                for b in range(B):
                    dve.scalar_tensor_tensor(out=m_lo[:, b], in0=ma_ps[:, b], scalar=recips[:, r, 0, b:b + 1],
                                             in1=read(m_hi[:, b]), op0=ALU.mult,
                                             op1=ALU.subtract).then_inc(mlo_made, 1)

            def cut_a(n):
                dve.wait_ge(ahi_made, n + 1)
                dve.tensor_tensor(a_lo[:], ma_ps[:], read(a_hi[:]), ALU.subtract).then_inc(alo_made, 1)

            def scale_z(n, r, b):
                dve.wait_ge(dn_made, n + 1)
                dve.wait_ge(z_done, B * n + b + 1)
                dve.scalar_tensor_tensor(out=pre[:, b], in0=z_ps[:, b], scalar=dn[:, r, b:b + 1],
                                         in1=b1_all[:], op0=ALU.mult, op1=ALU.add).then_inc(pre_made, 1)

            def hidden_stats(n, b):
                dve.wait_ge(relu_made, B * n + b + 1)
                dve.bn_stats(bn_h[:, b], act_h[:, b]).then_inc(bnh_made, 1)

            def hidden_moments(n, b):
                k = settled(dve, B * n + b + 1)
                dve.wait_ge(ident_made, 1)
                dve.wait_ge(bnh_made, k)
                dve.bn_aggr(mv_h[:, b], bn_h[:, b]).then_inc(mvh_made, 1)

            def cut_t(n, b):
                dve.wait_ge(thi_made, B * n + b + 1)
                dve.tensor_tensor(t_lo[:, b], t_ps[:, b], read(t_hi[:, b]), ALU.subtract).then_inc(tlo_made, 1)

            def add_bias(n):
                dve.wait_ge(y_done, n + 1)
                dve.tensor_tensor(y_sum[:], y_ps[:], beta_w2[:], ALU.add).then_inc(ysum_made, 1)

            def cut_p(n, r, p, hi, lo):
                dve.wait_ge(phi_made, B * (n + 1))
                for b in range(B):
                    dve.scalar_tensor_tensor(out=lo[:, b], in0=p[:, b], scalar=recips[:, r, 0, b:b + 1],
                                             in1=read(hi[:, b]), op0=ALU.mult,
                                             op1=ALU.subtract).then_inc(plo_made, 1)

            def add_up(n, r, q, b, o):
                if b == 0:
                    dve.wait_ge(o_done, n + 1)
                    dve.wait_ge(skip_made, n + 1)
                    if not isinstance(n, int) or n > 1:
                        dve.wait_ge(fin_made, B * (n - 1))
                dve.scalar_tensor_tensor(out=res[:, q, b], in0=o[:, b], scalar=dn[:, r, b:b + 1],
                                         in1=skip[:, r, b], op0=ALU.mult, op1=ALU.add).then_inc(res_made, 1)

            def out_stats(n, q, b):
                dve.wait_ge(res_made, B * n + b + 1)
                dve.bn_stats(bn_o[:, q, b], res[:, q, b]).then_inc(bno_made, 1)

            def out_moments(n, q):
                k = settled(dve, B * (n + 1))
                dve.wait_ge(ident_made, 1)
                dve.wait_ge(bno_made, k)
                for b in range(B):
                    dve.bn_aggr(mv_o[:, q, b], bn_o[:, q, b]).then_inc(mvo_made, 1)

            def keep_w2():
                for b in range(B):
                    dve.wait_ge(w2_turned, b + 1)
                    dve.tensor_copy(w2t[:, :, b * P:(b + 1) * P], t_ps[:, b]).then_inc(w2_kept, 1)

            def spread_beta():
                dve.wait_ge(scales_in, 32)
                for b in range(HB):
                    dve.tensor_scalar(beta_wide[:, b], ones[:], beta_col[:, b:b + 1], None,
                                      ALU.mult).then_inc(beta_spread, 1)

            def cut_w2_and_bias():
                for b in range(HB):
                    dve.wait_ge(w2hi_made, b + 1)
                    dve.scalar_tensor_tensor(out=w2g_lo[:, b], in0=w2t[:, b], scalar=gamma_col[:, b:b + 1],
                                             in1=read(w2g_hi[:, b]), op0=ALU.mult,
                                             op1=ALU.subtract).then_inc(w2lo_made, 1)
                dve.wait_ge(bias_done, 1)
                for b in range(B):
                    dve.tensor_copy(beta_w2[:, b], y_ps[:, 0]).then_inc(bias_kept, 1)
                dve.wait_ge(bias_kept, B)

            def step(i, c, j, two_after=True, after=True, before=True, two_before=True, three_before=True,
                     setup=False):
                this, behind, ahead, far, q = c % RING, (c - 2) % RING, (c + 1) % RING, (c + 2) % RING, c % 2
                scale_z(i, this, 0)
                if three_before:
                    out_moments(i - 3, (c - 3) % 2)
                if setup:
                    spread_beta()
                if before:
                    cut_t(i - 1, 0)
                scale_z(i, this, 1)
                hidden_stats(i, 0)
                if before and after:
                    cut_t(i - 1, 1)
                if after:
                    clamp_counts(i + 1, ahead)
                hidden_moments(i, 0)
                if after:
                    invert_counts(i + 1, ahead)
                hidden_stats(i, 1)
                if after:
                    cut_m(i + 1, ahead)
                hidden_moments(i, 1)
                if not after:
                    cut_t(i - 1, 1)
                if two_before:
                    cut_p(i - 2, behind, po_ps, p_hi, p_lo)
                if before:
                    add_bias(i - 1)
                if two_after:
                    make_h(i + 2, far, 16 * (j + (c + 2) // RING + 1))
                if after:
                    cut_a(i + 1)
                    sum_degrees(i + 1, ahead)
                if two_before:
                    add_up(i - 2, behind, q, 0, po_ps)
                if after:
                    clamp_degrees(i + 1, ahead)
                if two_before:
                    add_up(i - 2, behind, q, 1, po_ps)
                if after:
                    invert_degrees(i + 1, ahead)
                else:
                    cut_t(i, 0)
                    cut_t(i, 1)
                if two_before:
                    out_stats(i - 2, q, 0)
                if after:
                    node_scale(i + 1, ahead)
                if setup:
                    cut_w2_and_bias()
                if two_before:
                    out_stats(i - 2, q, 1)

            dve.wait_ge(setup_pool, 4)
            dve.tensor_copy(ident_16[:], ident[:]).then_inc(ident_made, 1)
            make_h(0, 0, 16)
            dve.wait_ge(xhi_made, 1)
            dve.tensor_tensor(x_lo[:], x_in[:, 0], read(x_hi[:]), ALU.subtract).then_inc(xlo_made, 1)
            clamp_counts(0, 0)
            dve.wait_ge(row0_turned, 1)
            turned = y_ps[:, :, 0:N]
            dve.tensor_copy(row0_cut[:, :, :, 0], turned).then_inc(row0_steps, 1)
            invert_counts(0, 0)
            dve.wait_ge(row0_steps, 1)
            dve.tensor_tensor(row0_rest[:, :, 0], turned, row0_cut[:, :, :, 0], ALU.subtract).then_inc(row0_steps, 1)
            dve.wait_ge(row0_steps, 2)
            dve.tensor_copy(row0_cut[:, :, :, 1], row0_rest[:, :, 0]).then_inc(row0_steps, 1)
            dve.wait_ge(row0_steps, 3)
            dve.tensor_tensor(row0_rest[:, :, 1], row0_rest[:, :, 0], row0_cut[:, :, :, 1],
                              ALU.subtract).then_inc(row0_steps, 1)
            dve.wait_ge(row0_steps, 4)
            dve.tensor_copy(row0_cut[:, :, :, 2], row0_rest[:, :, 1]).then_inc(row0_steps, 1)
            cut_m(0, 0)
            make_h(1, 1, 16)
            for b in range(B):
                dve.wait_ge(w1hi_made, b + 1)
                dve.tensor_tensor(w1t_lo[:, b], z_ps[:, b], read(w1t_hi[:, b]), ALU.subtract).then_inc(w1lo_made, 1)
            cut_a(0)
            sum_degrees(0, 0)
            clamp_degrees(0, 0)
            invert_degrees(0, 0)
            node_scale(0, 0)
            keep_w2()
            dve.wait_ge(b1_in, 16)
            step(0, 0, 0, before=False, two_before=False, three_before=False, setup=True)
            for i in range(1, FIRST):
                step(i, i, 0, two_before=i >= 2, three_before=i >= 3)
            with dve.Fori(0, LOOPS) as j:
                for c in range(FIRST, FIRST + RING):
                    step(RING * j + c, c, j)
            for i in range(LAST, N):
                step(i, i, 0, two_after=i + 2 < N, after=i + 1 < N)
            out_moments(N - 3, (N - 3) % 2)
            dve.wait_ge(ylo_made, N - 1)
            add_bias(N - 1)
            dve.wait_ge(yhi_made, N)
            dve.tensor_tensor(y_lo[:], y_sum[:], read(y_hi[:]), ALU.subtract).then_inc(ylo_made, 1)
            cut_p(N - 2, (N - 2) % RING, po_ps, p_hi, p_lo)
            cut_p(N - 1, (N - 1) % RING, last_po_ps, last_p_hi, last_p_lo)
            for n, o in ((N - 2, po_ps), (N - 1, last_po_ps)):
                for b in range(B):
                    add_up(n, n % RING, n % 2, b, o)
                for b in range(B):
                    out_stats(n, n % 2, b)
                out_moments(n, n % 2)

        @block.tensor
        def _(pe):
            def product(out, pairs, start=True, stop=True):
                for k, (lhs, rhs) in enumerate(pairs):
                    mm = pe.matmul(out, lhs, rhs, start=start and k == 0, stop=stop and k == len(pairs) - 1)
                return mm

            def turn_h(n, r, reused):
                pe.wait_ge(h16_made, n + 1)
                if reused:
                    pe.wait_ge(deg_summed, n)
                for e in range(B):
                    for b in range(B):
                        mm = product(ht_ps[:, e, b * P:(b + 1) * P], [(H16[:, b, e * P:(e + 1) * P], ident_16[:])])
                mm.then_inc(ht_turned, 1)

            def edge_sums(n, r):
                pe.wait_ge(xhi_made, n + 1)
                pe.wait_ge(xlo_made, n + 1)
                for e in range(B):
                    mm = product(ma_ps[:, e], [(H[:, r, b, e * P:(e + 1) * P], part[:, b])
                                               for part in (x_hi, x_lo) for b in range(B)])
                mm.then_inc(m_done, 1)

            def degrees(n, r):
                pe.wait_ge(row0_copied, n + 1)
                pe.wait_ge(ht16_made, n + 1)
                for b in range(B):
                    mm = product(ht_ps[:, b, 0:PARTS], [(HT16[:, e, b * P:(b + 1) * P], row0_now[:, r, e])
                                                        for e in range(B)])
                mm.then_inc(deg_done, 1)

            def node_sums(n, r):
                pe.wait_ge(mhi_made, B * (n + 1))
                pe.wait_ge(mlo_made, B * (n + 1))
                for d in range(B):
                    mm = product(ma_ps[:, d], [(part[:, e, d * P:(d + 1) * P], HT[:, r, e])
                                               for part in (m_hi, m_lo) for e in range(B)])
                mm.then_inc(a_done, 1)

            def hidden(n, reused):
                pe.wait_ge(ahi_made, n + 1)
                pe.wait_ge(alo_made, n + 1)
                for b in range(B):
                    if reused:
                        pe.wait_ge(pre_made, B * n + b - 1)
                    mm = product(z_ps[:, b], [(a[:, d, b * P:(b + 1) * P], w[:, d])
                                              for a, w in ((a_hi, w1t_hi), (a_hi, w1t_lo), (a_lo, w1t_hi))
                                              for d in range(B)])
                    mm.then_inc(z_done, 1)

            def turn_t(n, b):
                pe.wait_ge(norm_made, B * n + b + 1)
                for h in range(HB):
                    mm = pe.transpose(t_ps[:, b, h], norm_h[:, b, h * P:(h + 1) * P], ident[:])
                mm.then_inc(t_turned, 1)

            def project(n):
                for b in range(B):
                    pe.wait_ge(thi_made, B * n + b + 1)
                    product(y_ps[:, b], [(t_hi[:, b, h], w[:, h]) for w in (w2g_hi, w2g_lo) for h in range(HB)],
                            stop=False)
                    pe.wait_ge(tlo_made, B * n + b + 1)
                    mm = product(y_ps[:, b], [(t_lo[:, b, h], w2g_hi[:, h]) for h in range(HB)], start=False)
                mm.then_inc(y_done, 1)

            def edge_sums_2(n, r, p, reused):
                pe.wait_ge(yhi_made, n + 1)
                pe.wait_ge(ylo_made, n + 1)
                if reused:
                    pe.wait_ge(res_made, B * n)
                for e in range(B):
                    mm = product(p[:, e], [(H[:, r, b, e * P:(e + 1) * P], part[:, b])
                                           for part in (y_hi, y_lo) for b in range(B)])
                mm.then_inc(p_done, 1)

            def node_sums_2(n, r, o, hi, lo):
                pe.wait_ge(phi_made, B * (n + 1))
                pe.wait_ge(plo_made, B * (n + 1))
                for b in range(B):
                    mm = product(o[:, b], [(HT[:, r, e, b * P:(b + 1) * P], part[:, e])
                                           for part in (hi, lo) for e in range(B)])
                mm.then_inc(o_done, 1)

            def turn_w2():
                pe.wait_ge(w2_in, 16)
                for b in range(B):
                    for h in range(HB):
                        mm = pe.transpose(t_ps[:, b, h], w2_nat[:, b, h * P:(h + 1) * P], ident[:])
                    mm.then_inc(w2_turned, 1)

            def step(i, c, after=True, before=True, two_before=True, setup=False):
                peeled = isinstance(i, int)
                behind, ahead = (c - 2) % RING, (c + 1) % RING
                hidden(i, not peeled or i > 0)
                if two_before:
                    edge_sums_2(i - 2, behind, po_ps, not peeled or i > 2)
                if after:
                    turn_h(i + 1, ahead, True)
                    edge_sums(i + 1, ahead)
                if setup:
                    pe.wait_ge(w2_kept, B)
                    pe.wait_ge(beta_spread, HB)
                    product(y_ps[:, 0], [(beta_wide[:, h], w2t[:, h]) for h in range(HB)]).then_inc(bias_done, 1)
                if before:
                    if peeled and i == 1:
                        pe.wait_ge(w2lo_made, HB)
                        pe.wait_ge(bias_kept, B)
                    project(i - 1)
                if after:
                    node_sums(i + 1, ahead)
                if two_before:
                    node_sums_2(i - 2, behind, po_ps, p_hi, p_lo)
                if after:
                    degrees(i + 1, ahead)
                turn_t(i, 0)
                turn_t(i, 1)

            pe.wait_ge(setup_pool, 4)
            pe.wait_ge(ident_made, 1)
            turn_h(0, 0, False)
            pe.wait_ge(row0_in, 16)
            for b in range(B):
                mm = pe.transpose(y_ps[:, b, 0:N], row0_nat[:, b * P:(b + 1) * P], ident[0:N, 0:N])
            mm.then_inc(row0_turned, 1)
            edge_sums(0, 0)
            pe.wait_ge(w1_in, 16)
            for b in range(B):
                for h in range(HB):
                    mm = pe.transpose(z_ps[:, b, h * P:(h + 1) * P], w1_nat[:, h, b * P:(b + 1) * P], ident[:])
                mm.then_inc(w1_turned, 1)
            node_sums(0, 0)
            degrees(0, 0)
            turn_w2()
            pe.wait_ge(w1lo_made, B)
            step(0, 0, before=False, two_before=False, setup=True)
            for i in range(1, FIRST):
                step(i, i, two_before=i >= 2)
            with pe.Fori(0, LOOPS) as j:
                for c in range(FIRST, FIRST + RING):
                    step(RING * j + c, c)
            for i in range(LAST, N):
                step(i, i, after=i + 1 < N)
            pe.wait_ge(ysum_made, N - 1)
            project(N - 1)
            edge_sums_2(N - 2, (N - 2) % RING, po_ps, True)
            edge_sums_2(N - 1, (N - 1) % RING, last_po_ps, False)
            node_sums_2(N - 2, (N - 2) % RING, po_ps, p_hi, p_lo)
            node_sums_2(N - 1, (N - 1) % RING, last_po_ps, last_p_hi, last_p_lo)


_INS = ["x", "adj", "L0_gnn_W1", "L0_gnn_b1", "L0_gnn_gamma", "L0_gnn_beta", "L0_gnn_W2", "L0_gnn_b2"]


def kernel(**inputs):
    import numpy as _np
    import concourse.bacc as _bacc
    from concourse import mybir as _mybir
    from concourse.bass_utils import run_bass_kernel_spmd as _run

    nc = _bacc.Bacc("TRN2", target_bir_lowering=False, num_devices=1)
    arrays, args = {}, []
    for name in _INS:
        a = _np.ascontiguousarray(inputs[name])
        arrays[f"in_{name}"] = a
        args.append(nc.dram_tensor(f"in_{name}", a.shape, _mybir.dt.from_np(a.dtype), kind="ExternalInput").ap())
    shape = arrays["in_x"].shape
    out = nc.dram_tensor("out_0", shape, _mybir.dt.float32, kind="ExternalOutput").ap()
    hypergraph_kernel(nc, *args, out)
    r = _run(nc, [arrays], core_ids=[0])
    return r.results[0]["out_0"]
```
